# Optimizing a Trainium2 kernel written in Bass

```python
import numpy as np
import jax
import jax.numpy as jnp

def _softmax(x, axis=-1):
    return jax.nn.softmax(x, axis=axis)

def _gelu(x):
    return jax.nn.gelu(x, approximate=True)

def _silu(x):
    return jax.nn.silu(x)

def _sigmoid(x):
    return jax.nn.sigmoid(x)

def _layernorm(x, axis=-1, eps=1e-05):
    m = jnp.mean(x, axis=axis, keepdims=True)
    v = jnp.var(x, axis=axis, keepdims=True)
    return (x - m) / jnp.sqrt(v + eps)

def _scatter_add(tgt, idx, src, axis=0):
    return tgt.at[idx].add(src)

def _segment_sum(src, seg, n):
    return jax.ops.segment_sum(src, seg, n)
kernel_name = 'mk_flamingo_gated_d1_seqx_r8_186647'

def setup_inputs(seed: int=0):
    np.random.seed(seed)
    _w = jnp.asarray

    def _rec_inputs():
        import jax
        import jax.numpy as jnp
        _rk = jax.random.key(seed)
        x = -0.0003929 + 0.9999 * jax.random.normal(jax.random.fold_in(_rk, 1), (32, 128, 128), jnp.float32)
        _lenS = 128 - jax.random.randint(jax.random.fold_in(_rk, 7), (32,), 0, max(1, 128 // 4) + 1, jnp.int32)
        _lenS2 = 77 - jax.random.randint(jax.random.fold_in(_rk, 8), (32,), 0, max(1, 77 // 4) + 1, jnp.int32)
        _ctx_768P = jax.random.normal(jax.random.fold_in(_rk, 11), (32, 16, 96), jnp.float32)
        _ctx_768c = jax.random.dirichlet(jax.random.fold_in(_rk, 511), 0.3 * jnp.ones((16,), jnp.float32), (32, 77))
        _ctx_768t = jnp.einsum('bsk,bkd->bsd', _ctx_768c, _ctx_768P)
        _ctx_768t = _ctx_768t * jax.lax.rsqrt(jnp.mean(jnp.square(_ctx_768t)) + 1e-12) * 0.953939
        ctx_768 = -0.00055796 + 0.999787 * (_ctx_768t + 0.3 * jax.random.normal(jax.random.fold_in(_rk, 611), (32, 77, 96), jnp.float32))
        _g = jax.random.normal(jax.random.fold_in(_rk, 9001), (2, 1), jnp.float32)
        _g = jnp.sign(_g) * jnp.maximum(jnp.abs(_g), 1.0) + (_g == 0) * 1.0
        g_xattn = _g[0]
        g_ffn = _g[1]
        return (x, ctx_768, g_xattn, g_ffn)
    x, ctx_768, g_xattn, g_ffn = _rec_inputs()

    def _L0_xattn_setup():
        import jax, jax.numpy as jnp
        import numpy as np
        D = 128
        L = 96
        H = 16
        EPS = 1e-05

        def layer_norm(x, g, b):
            mu = jnp.mean(x, axis=-1, keepdims=True)
            var = jnp.var(x, axis=-1, keepdims=True)
            return (x - mu) * jax.lax.rsqrt(var + EPS) * g + b
        key = jax.random.key(seed)
        ks = jax.random.split(key, 8)
        B, T, N = (4, 512, 64)
        sq = lambda d: 1.0 / np.sqrt(d)
        return {'x': jax.random.normal(ks[0], (B, T, D), jnp.float32), 'xf': jax.random.normal(ks[1], (B, N, L), jnp.float32), 'norm_g': jnp.ones((D,), jnp.float32), 'norm_b': jnp.zeros((D,), jnp.float32), 'tnorm_g': jnp.ones((L,), jnp.float32), 'tnorm_b': jnp.zeros((L,), jnp.float32), 'Wq': jax.random.normal(ks[2], (D, D), jnp.float32) * sq(D), 'bq': jnp.zeros((D,), jnp.float32), 'Wk': jax.random.normal(ks[3], (L, D), jnp.float32) * sq(L), 'bk': jnp.zeros((D,), jnp.float32), 'Wv': jax.random.normal(ks[4], (L, D), jnp.float32) * sq(L), 'bv': jnp.zeros((D,), jnp.float32)}
    _L0_xattn_all = _L0_xattn_setup()
    _L0_xattn_in = {k: v for k, v in _L0_xattn_all.items() if k in ('norm_g', 'norm_b', 'tnorm_g', 'tnorm_b', 'Wq', 'bq', 'Wk', 'bk', 'Wv', 'bv')}
    del _L0_xattn_all

    def _L0_ffn_setup():
        import jax, jax.numpy as jnp
        import numpy as np
        TOP_K = 2
        key = jax.random.key(seed)
        k0, k1, k2, k3 = jax.random.split(key, 4)
        B, T, C, E, D = (4, 256, 128, 8, 128)
        x = jax.random.normal(k0, (B, T, C), dtype=jnp.float32)
        s = 1.0 / np.sqrt(C)
        w_router = jax.random.normal(k1, (C, E), dtype=jnp.float32) * s
        w1 = jax.random.normal(k2, (E, C, D), dtype=jnp.float32) * s
        w2 = jax.random.normal(k3, (E, D, C), dtype=jnp.float32) * (1.0 / np.sqrt(D))
        return {'x': x, 'w_router': w_router, 'w1': w1, 'w2': w2}
    _L0_ffn_all = _L0_ffn_setup()
    _L0_ffn_in = {k: v for k, v in _L0_ffn_all.items() if k in ('w_router', 'w1', 'w2')}
    del _L0_ffn_all
    return {'x': x, 'ctx_768': ctx_768, 'g_xattn': g_xattn, 'g_ffn': g_ffn, 'L0_xattn_norm_g': _L0_xattn_in['norm_g'], 'L0_xattn_norm_b': _L0_xattn_in['norm_b'], 'L0_xattn_tnorm_g': _L0_xattn_in['tnorm_g'], 'L0_xattn_tnorm_b': _L0_xattn_in['tnorm_b'], 'L0_xattn_Wq': _L0_xattn_in['Wq'], 'L0_xattn_bq': _L0_xattn_in['bq'], 'L0_xattn_Wk': _L0_xattn_in['Wk'], 'L0_xattn_bk': _L0_xattn_in['bk'], 'L0_xattn_Wv': _L0_xattn_in['Wv'], 'L0_xattn_bv': _L0_xattn_in['bv'], 'L0_ffn_w_router': _L0_ffn_in['w_router'], 'L0_ffn_w1': _L0_ffn_in['w1'], 'L0_ffn_w2': _L0_ffn_in['w2']}

def reference(x, ctx_768, g_xattn, g_ffn, L0_xattn_norm_g, L0_xattn_norm_b, L0_xattn_tnorm_g, L0_xattn_tnorm_b, L0_xattn_Wq, L0_xattn_bq, L0_xattn_Wk, L0_xattn_bk, L0_xattn_Wv, L0_xattn_bv, L0_ffn_w_router, L0_ffn_w1, L0_ffn_w2):
    import jax
    import jax.numpy as jnp

    def _L0_xattn_ref(x, xf, norm_g, norm_b, tnorm_g, tnorm_b, Wq, bq, Wk, bk, Wv, bv):
        import jax, jax.numpy as jnp
        import numpy as np
        D = 128
        L = 96
        H = 16
        EPS = 1e-05

        def layer_norm(x, g, b):
            mu = jnp.mean(x, axis=-1, keepdims=True)
            var = jnp.var(x, axis=-1, keepdims=True)
            return (x - mu) * jax.lax.rsqrt(var + EPS) * g + b
        B, T, _ = x.shape
        N = xf.shape[1]
        hd = D // H
        xn = layer_norm(x, norm_g, norm_b)
        xfn = layer_norm(xf, tnorm_g, tnorm_b)
        q = (xn @ Wq + bq).reshape(B, T, H, hd)
        k = (xfn @ Wk + bk).reshape(B, N, H, hd)
        v = (xfn @ Wv + bv).reshape(B, N, H, hd)
        scores = jnp.einsum('bthd,bnhd->bhtn', q, k) / jnp.sqrt(jnp.float32(hd))
        w = jax.nn.softmax(scores, axis=-1)
        y = jnp.einsum('bhtn,bnhd->bthd', w, v).reshape(B, T, D)
        return y

    def _L0_ffn_ref(x, w_router, w1, w2):
        import jax, jax.numpy as jnp
        import numpy as np
        TOP_K = 2
        B, T, C = x.shape
        xf = x.reshape(-1, C)
        logits = xf @ w_router
        top_vals, top_idx = jax.lax.top_k(logits, TOP_K)
        probs = jax.nn.softmax(top_vals, axis=-1)
        h = jnp.square(jax.nn.relu(jnp.einsum('nc,ecd->ned', xf, w1)))
        y_all = jnp.einsum('ned,edc->nec', h, w2)
        y_sel = jnp.take_along_axis(y_all, top_idx[:, :, None], axis=1)
        out = jnp.sum(y_sel * probs[:, :, None], axis=1)
        return out.reshape(B, T, C)
    x = x + jnp.tanh(g_xattn[0]) * _L0_xattn_ref(_layernorm(x, axis=-1), ctx_768, L0_xattn_norm_g, L0_xattn_norm_b, L0_xattn_tnorm_g, L0_xattn_tnorm_b, L0_xattn_Wq, L0_xattn_bq, L0_xattn_Wk, L0_xattn_bk, L0_xattn_Wv, L0_xattn_bv)
    x = x + jnp.tanh(g_ffn[0]) * _L0_ffn_ref(_layernorm(x, axis=-1), L0_ffn_w_router, L0_ffn_w1, L0_ffn_w2)
    return x

_drawn_inputs = setup_inputs


def setup_inputs(seed=0):
    import zlib

    import numpy as np

    out = dict(_drawn_inputs(seed))
    spreads = {'L0_xattn_norm_g': (1.0, 0.2),
     'L0_xattn_norm_b': (0.0, 0.1),
     'L0_xattn_tnorm_g': (1.0, 0.2),
     'L0_xattn_tnorm_b': (0.0, 0.1),
     'L0_xattn_bq': (0.0, 0.1),
     'L0_xattn_bk': (0.0, 0.1),
     'L0_xattn_bv': (0.0, 0.1)}
    factors = {}
    for name, (base, spread) in spreads.items():
        noise = np.random.default_rng([zlib.crc32(name.encode()), seed]).standard_normal(out[name].shape)
        drawn = base * np.exp(spread * noise) if base else spread * noise
        out[name] = jnp.asarray(drawn.astype(out[name].dtype))
    for name, factor in factors.items():
        out[name] = (out[name] * factor).astype(out[name].dtype)
    return out
```

```python
from contextlib import ExitStack

import concourse.bass as bass
from concourse import mybir

ALU = mybir.AluOpType
ACT = mybir.ActivationFunctionType
AX = mybir.AxisListType
F32 = mybir.dt.float32
F32R = mybir.dt.float32r
BF16 = mybir.dt.bfloat16
F16 = mybir.dt.float16
U32 = mybir.dt.uint32

G = 4
PARTS = 3
TERMS = PARTS * PARTS
HEADS_S1 = [(0, 6), (6, 12), (12, 16)]
CH = 4
SLOTS = 4
EPS = 1e-5


def landed(s, par, dmas=1):
    return dmas * (8 * (s - par) + 16)


def at(steps, n, name):
    return len(steps) * n + steps.index(name) + 1


AB_USES = ["ctxT", "xT", "k", "v0", "v1", "q"] + [f"{u}{j}" for j in range(G) for u in ("s1a", "s1b", "s1c", "mT")]
AB_HALF = len(AB_USES) // 2

NORM = ["ctx_stats", "x_stats", "ctx_moments", "x_moments", "ctx_normed", "x_normed"]
NORM_P = ["var_eps", "rstd1", "v_r", "v_rr", "v2_eps", "rstd2", "rstd", "cvar_eps", "crstd"]
SPLIT_QK = ["hi", "rest", "mid", "lo"]
SPLIT_V = ["hi", "rest", "mid", "lo"]
MAXP = ["hi", "rest", "mid", "lo"]
POST = ["summed", "recip", "scaled", "x1", "stats", "moments", "normed", "xT", "x_hi", "x_lo", "logits", "top", "index"]
POST_P = ["var_eps", "rstd"]
GATE = ["diff", "den", "p1", "p2", "idx_f", "eq1", "eq2", "g1", "g2", "gates", "gT"]


def flamingo_kernel(nc, x, ctx, g_xattn, g_ffn, norm_g, norm_b, tnorm_g, tnorm_b,
                    Wq, bq, Wk, bk, Wv, bv, w_router, w1, w2, out):
    B, T, D = x.shape
    N, L = ctx.shape[1:]
    E = w_router.shape[1]
    H = 16
    HD = D // H
    S = B // G
    GT = G * T
    QR = TERMS * HD
    MR = QR + PARTS
    NC = H // CH
    VC = HD * PARTS + 1
    SCALE = float(HD) ** -0.5
    assert T == 128 and D == 128 and S % 2 == 0 and S >= 6 and E == 8

    x_v = x.rearrange("(s g) t d -> s t g d", g=G)
    ctx_v = ctx.rearrange("(s g) n l -> s n g l", g=G)
    out_v = out.rearrange("(s g) t d -> s t g d", g=G)
    gates_dram = nc.dram_tensor("gates_scratch", [2, E, G, T], F32, kind="Internal").ap()

    with ExitStack() as stack:
        def sb(name, shape, dt=F32):
            return stack.enter_context(nc.sbuf_tensor(name, shape, dt))

        def sem(name):
            return stack.enter_context(nc.semaphore(name))

        def sems(name, n):
            return [sem(f"{name}{i}") for i in range(n)]

        ident = sb("ident", [128, 128])
        ident_bf = sb("ident_bf", [128, 128], BF16)
        half = sb("half", [128, 2 * G])
        neg_half = sb("neg_half", [128, G])
        iota = sb("iota", [128, G, E])
        wq_in = sb("wq_in", [D, D])
        wk_in = sb("wk_in", [L, D])
        wq = sb("wq", [D, D])
        wk = sb("wk", [L, D])
        wv = sb("wv", [L + 1, D])
        wr = sb("wr", [D, E])
        w1_in = sb("w1_in", [D, E, D])
        w2_in = sb("w2_in", [D, E, D])
        w1_hi = sb("w1_hi", [D, E, D], F32R)
        w1_lo = sb("w1_lo", [D, E, D], F32R)
        w2s = sb("w2s", [D, E, D])
        vec = sb("vec", [128, 10])
        CONSTS, ONES = 12, 3
        WEIGHTS = ONES + 7
        NG, NB_, BQ, BK, TG, TB, GX, GF, BQS = range(9)

        def col(i, n=128):
            return vec[0:n, i:i + 1]

        x_sb = sb("x_sb", [T, 2, G, D])
        ctx_sb = sb("ctx_sb", [N, 2, G, L])
        x_res = sb("x_res", [T, 2, G, D])
        x_st = sb("x_st", [T, G, 6])
        c_st = sb("c_st", [N, G, 6])
        x_mv = sb("x_mv", [T, G, 2])
        c_mv = sb("c_mv", [N, G, 2])
        nrm = sb("nrm", [T, 8, G])
        xn = sb("xn", [T, G, D])
        cn = sb("cn", [N, G, L])
        xnT = sb("xnT", [D, GT])
        cnT = sb("cnT", [L + 1, G * N])
        q32 = sb("q32", [D, GT])
        k32 = sb("k32", [D, G * N])
        v32 = sb("v32", [N, G, D])
        q_rest = sb("q_rest", [D, GT])
        k_rest = sb("k_rest", [D, G * N])
        v_rest = sb("v_rest", [N, G, D])
        q_parts = sb("q_parts", [D, PARTS, GT], BF16)
        k_parts = sb("k_parts", [D, PARTS, G * N], BF16)
        qs = sb("qs", [MR, 2, H, GT], BF16)
        ks = sb("ks", [MR, 2, H, G * N], BF16)
        vs = sb("vs", [N, 2, G, H, VC], BF16)
        negm = sb("negm", [T, H])
        m_rest = sb("m_rest", [T, H])
        m_parts = sb("m_parts", [T, PARTS, H], BF16)
        mT = sb("mT", [PARTS * H, 2, T], BF16)
        LR = NC
        p32 = sb("p32", [N, LR, CH * T])
        p_hi = sb("p_hi", [N, LR, CH * T], F16)
        p_lo = sb("p_lo", [N, LR, CH * T], F16)
        o = sb("o", [T, D])
        rden = sb("rden", [T, H])
        x1 = sb("x1", [T, 2, G, D])
        st2 = sb("st2", [T, 6])
        mv2 = sb("mv2", [T, 2])
        rs2 = sb("rs2", [T, 2])
        xn2 = sb("xn2", [T, D])
        xT32 = sb("xT32", [D, 2, T])
        x_hi = sb("x_hi", [D, 2, GT], F32R)
        x_lo = sb("x_lo", [D, 2, GT], F32R)
        logits = sb("logits", [T, G, E])
        top = sb("top", [T, G, E])
        index = sb("index", [T, G, E], U32)
        gt = sb("gt", [T, 8, G])
        gate_s = sb("gate_s", [T, 2, G])
        idx_f = sb("idx_f", [T, G, 2])
        eq1 = sb("eq1", [T, G, E])
        eq2 = sb("eq2", [T, G, E])
        gates = sb("gates", [T, G, E])
        gatesT = sb("gatesT", [G * E, T])
        gb = sb("gb", [D, 2, E, GT])
        u = sb("u", [D, 2, GT])
        hs = sb("hs", [D, 2, GT])
        y_out = sb("y_out", [T, 2, G, D])

        def ps(name):
            return stack.enter_context(nc.psum_tensor(name, [128, 512], F32))

        bank_s2 = [ps("s2_0"), ps("s2_1")]
        bank_h = [ps("h_0"), ps("h_1")]
        bank_y = ps("y")
        bank_c = ps("c")
        bank_ab = [ps("ab_0"), ps("ab_1")]

        w_in = sem("w_in")
        const_made = sem("const_made")
        w_made = sem("w_made")
        tanh_done = sem("tanh_done")
        x_in, ctx_in, res_in = sems("x_in", 2), sems("ctx_in", 2), sems("res_in", 2)
        ab_ready, ab_taken = sems("ab_ready", 2), sems("ab_taken", 2)
        norm_d, norm_p = sem("norm_d"), sem("norm_p")
        split_q, split_k, split_v = sem("split_q"), sem("split_k"), sem("split_v")
        q_stacked, k_stacked = sems("q_stacked", 2), sems("k_stacked", 2)
        ones_in = sem("ones_in")
        max_d = sem("max_d")
        m_in = sems("m_in", G)
        s2_ready = sem("s2_ready")
        hi_done, p_done, lo_done = sem("hi_done"), sem("p_done"), sem("lo_done")
        pv_done = sem("pv_done")
        post_d, post_p, post_t, post_l = sem("post_d"), sem("post_p"), sem("post_t"), sem("post_l")
        gate_d, gate_e, gate_p, gate_t = sem("gate_d"), sem("gate_e"), sem("gate_p"), sem("gate_t")
        g_stored, g_in = sems("g_stored", 2), sems("g_in", 2)
        h_ready, u_done, hs_done, y_done = sem("h_ready"), sem("u_done"), sem("hs_done"), sem("y_done")
        y_added = sem("y_added")
        stored = sems("stored", 2)

        held_apart = sem("held_apart")

        block = stack.enter_context(nc.Block())

        def apart(eng):
            eng.sem_inc(held_apart, 1)

        def ab(s, name):
            k = AB_USES.index(name)
            return k % 2, AB_HALF * s + k // 2 + 1

        def steps(eng, step, tail):
            step(-1, 1)
            step(0, 0)
            step(1, 1)
            with eng.Fori(1, S // 2 - 1) as pair:
                step(2 * pair, 0, loop=True)
                step(2 * pair + 1, 1, loop=True)
            step(S - 2, 0)
            step(S - 1, 1)
            tail()

        def previous(i, j):
            return (i, j - 1) if j else (i - 1, G - 1)

        def ffn_units(i, j):
            return (i - 1, 1, (2 * j - 2, 2 * j - 1)) if j else (i - 2, 0, (E - 2, E - 1))

        def exists(t, loop=False):
            return loop or 0 <= t < S

        @block.sync
        def _(sp):
            def load(s, par, loop=False):
                if loop or s >= 2:
                    sp.wait_ge(norm_d, at(NORM, s - 2, "x_normed"))
                    apart(sp)
                sp.dma_start(ctx_sb[:, par], ctx_v[s]).then_inc(ctx_in[par], 16)
                sp.dma_start(x_sb[:, par], x_v[s]).then_inc(x_in[par], 16)

            def load_rows(s, par, loop=False):
                if loop or s >= 2:
                    sp.wait_ge(post_d, at(POST, G * (s - 2) + G - 1, "x1"))
                    apart(sp)
                sp.dma_start(x_res[:, par], x_v[s]).then_inc(res_in[par], 16)

            def stack_k(s, par, loop=False):
                sp.wait_ge(split_k, at(SPLIT_QK, s, "lo"))
                apart(sp)
                if loop or s >= 2:
                    sp.wait_ge(s2_ready, H // CH * G * (s - 1))
                for a in range(PARTS):
                    for b in range(PARTS):
                        r = HD * (PARTS * a + b)
                        sp.dma_start(ks[r:r + HD, par], k_parts[:, b, :]).then_inc(k_stacked[par], 16)

            def stack_q(s, par, loop=False):
                sp.wait_ge(split_q, at(SPLIT_QK, s, "lo"))
                for a in range(PARTS):
                    for b in range(PARTS):
                        r = HD * (PARTS * a + b)
                        sp.dma_start(qs[r:r + HD, par], q_parts[:, a, :]).then_inc(q_stacked[par], 16)

            def max_rows(s, par, j):
                bank, n = ab(s, f"mT{j}")
                sp.wait_ge(ab_taken[bank], n)
                sp.dma_start(qs[QR:MR, par, :, T * j:T * j + T], mT[:, j % 2, :]).then_inc(m_in[j], 16)

            def spread_gates(s, par):
                sp.wait_ge(gate_d, at(GATE, s, "gT"))
                for b in range(G):
                    sp.dma_start(gates_dram[par, :, b, :], gatesT[E * b:E * b + E, :]).then_inc(g_stored[par], 16)

            def spread_gates2(s, par, half_, loop=False):
                if half_ == 0:
                    sp.wait_ge(g_stored[par], landed(s, par, G))
                e0, e1 = (0, E // 2) if half_ == 0 else (E // 2, E)
                src = gates_dram[par, e0:e1].rearrange("e b t -> (e b t)").rearrange("(o n) -> o n", o=1)
                sp.dma_start(gb[:, par, e0:e1].rearrange("p e n -> p (e n)"),
                             src.broadcast_to([D, (e1 - e0) * GT])).then_inc(g_in[par], 16)

            def store(s, par):
                sp.wait_ge(y_added, s + 1)
                apart(sp)
                sp.dma_start(out_v[s], y_out[:, par]).then_inc(stored[par], 16)

            load(0, 0)
            for dst, src in ((wk_in[:, :], Wk), (wv[0:L, :], Wv), (wv[L:L + 1, :], bv.rearrange("(o n) -> o n", o=1)),
                             (wq_in[:, :], Wq), (col(NG), norm_g.rearrange("(n o) -> n o", o=1)),
                             (col(NB_), norm_b.rearrange("(n o) -> n o", o=1)),
                             (col(BQ), bq.rearrange("(h d o) -> d h o", d=HD, o=1)),
                             (col(BK), bk.rearrange("(h d o) -> d h o", d=HD, o=1)),
                             (col(TG, L), tnorm_g.rearrange("(n o) -> n o", o=1)),
                             (col(TB, L), tnorm_b.rearrange("(n o) -> n o", o=1)),
                             (col(GX), g_xattn.rearrange("(n o) -> n o", o=1).broadcast_to([128, 1])),
                             (col(GF), g_ffn.rearrange("(n o) -> n o", o=1).broadcast_to([128, 1])),
                             (wr[:, :], w_router),
                             (w1_in[:, :, :], w1.rearrange("e c d -> c e d")),
                             (w2_in[:, :, :], w2.rearrange("e d c -> d e c"))):
                with nc.allow_non_contiguous_dma(reason="short vectors"):
                    sp.dma_start(dst, src).then_inc(w_in, 16)

            def step(i, par, loop=False):
                nxt = i + 1
                more = loop or nxt < S
                if more:
                    if loop or nxt + 1 < S:
                        pass
                    load_rows(nxt, 1 - par, loop)
                if (loop or i >= 1):
                    spread_gates(i - 1, 1 - par)
                    spread_gates2(i - 1, 1 - par, 0, loop)
                    spread_gates2(i - 1, 1 - par, 1, loop)
                if more:
                    if not loop and i == -1:
                        sp.wait_ge(w_made, ONES)
                    stack_k(nxt, 1 - par, loop)
                    stack_q(nxt, 1 - par, loop)
                    if loop or nxt + 1 < S:
                        load(nxt + 1, par, loop)
                    for j in range(G):
                        max_rows(nxt, 1 - par, j)
                if loop or i >= 2:
                    store(i - 2, par)

            def tail():
                spread_gates(S - 1, 1)
                spread_gates2(S - 1, 1, 0)
                spread_gates2(S - 1, 1, 1)
                store(S - 2, 0)
                store(S - 1, 1)
                for par in range(2):
                    sp.wait_ge(stored[par], 16 * (S // 2 + 1))

            steps(sp, step, tail)

        @block.tensor
        def _(pe):
            def claim(s, name, loop=False):
                bank, n = ab(s, name)
                if loop or n > 1:
                    pe.wait_ge(ab_taken[bank], n - 1)
                return bank_ab[bank], ab_ready[bank]

            def transposes(s, loop=False):
                pe.wait_ge(norm_d, at(NORM, s, "ctx_normed"))
                p, ready = claim(s, "ctxT", loop)
                for b in range(G):
                    mm = nc.tensor.transpose(p[0:L, N * b:N * b + N], cn[:, b, :], ident[0:N, 0:N])
                mm.then_inc(ready, 1)
                pe.wait_ge(norm_d, at(NORM, s, "x_normed"))
                p, ready = claim(s, "xT", loop)
                for b in range(G):
                    mm = nc.tensor.transpose(p[:, T * b:T * b + T], xn[:, b, :], ident[:, :])
                mm.then_inc(ready, 1)

            def project(s, loop=False):
                bank, n = ab(s, "ctxT")
                pe.wait_ge(ab_taken[bank], n)
                p, ready = claim(s, "k", loop)
                nc.tensor.matmul(p[:, 0:G * N], wk[:, :], cnT[0:L, :], start=True, stop=True).then_inc(ready, 1)
                for half_ in range(2):
                    p, ready = claim(s, f"v{half_}", loop)
                    for b in range(2):
                        c = N * (2 * half_ + b)
                        mm = nc.tensor.matmul(p[0:N, D * b:D * b + D], cnT[:, c:c + N], wv[:, :],
                                              start=True, stop=True)
                    mm.then_inc(ready, 1)
                bank, n = ab(s, "xT")
                pe.wait_ge(ab_taken[bank], n)
                p, ready = claim(s, "q", loop)
                nc.tensor.matmul(p[:, :], wq[:, :], xnT[:, :], start=True, stop=True).then_inc(ready, 1)

            def stacked(s, par, loop=False):
                pe.wait_ge(k_stacked[par], landed(s, par, TERMS))
                pe.wait_ge(q_stacked[par], landed(s, par, TERMS))

            def scores(s, par, j, c, loop=False):
                if j == 0 and c == 0:
                    stacked(s, par, loop)
                h0, h1 = HEADS_S1[c]
                p, ready = claim(s, f"s1{'abc'[c]}{j}", loop)
                for h in range(h0, h1):
                    mm = nc.tensor.matmul(p[:, N * (h - h0):N * (h - h0 + 1)], qs[0:QR, par, h, T * j:T * j + T],
                                          ks[0:QR, par, h, N * j:N * j + N], start=True, stop=True)
                mm.then_inc(ready, 1)

            def max_turn(s, j, loop=False):
                pe.wait_ge(max_d, at(MAXP, G * s + j, "lo"))
                p, ready = claim(s, f"mT{j}", loop)
                apart(pe)
                nc.tensor.transpose(p[:, :].bitcast(BF16)[0:PARTS * H, 0:T],
                                    m_parts[:, :, :].rearrange("t a h -> t (a h)"), ident_bf[:, :]).then_inc(ready, 1)

            def scoresT(s, par, j, c, loop=False):
                if c == 0:
                    pe.wait_ge(m_in[j], 16 * s + 16)
                m = NC * (G * s + j) + c
                if loop or m >= 2:
                    pe.wait_ge(p_done, m - 1)
                p = bank_s2[c % 2]
                for h in range(CH * c, CH * c + CH):
                    mm = nc.tensor.matmul(p[0:N, T * (h - CH * c):T * (h - CH * c + 1)],
                                          ks[:, par, h, N * j:N * j + N], qs[:, par, h, T * j:T * j + T],
                                          start=True, stop=True)
                mm.then_inc(s2_ready, 1)

            def values(s, par, j, c, loop=False):
                n = G * s + j
                m = NC * n + c
                if c == 0:
                    pe.wait_ge(split_v, at(SPLIT_V, s, "lo"))
                    if loop or n > 0:
                        pe.wait_ge(post_d, at(POST, n - 1, "logits"))
                pe.wait_ge(lo_done, m + 1)
                for h in range(CH * c, CH * c + CH):
                    k = T * (h - CH * c)
                    for part in (p_hi, p_lo):
                        mm = nc.tensor.matmul(bank_c[:, VC * h:VC * h + VC], part[:, c, k:k + T],
                                              vs[:, par, j, h, :], start=(h == 0 and part is p_hi),
                                              stop=(part is p_lo), skip_group_check=True)
                mm.then_inc(pv_done, 1)

            def turn(n, par, j):
                pe.wait_ge(post_d, at(POST, n, "normed"))
                nc.tensor.transpose(bank_c[:, 0:T], xn2[:, :], ident[:, :]).then_inc(post_t, 1)

            def route(n, par, j):
                pe.wait_ge(post_d, at(POST, n, "xT"))
                nc.tensor.matmul(bank_c[:, 256:256 + E], xT32[:, j % 2, :], wr[:, :], start=True,
                                 stop=True).then_inc(post_l, 1)

            def gates_turn(s):
                pe.wait_ge(gate_d, at(GATE, s, "gates"))
                nc.tensor.transpose(bank_c[0:G * E, 0:T], gates[:, :, :].rearrange("t b e -> t (b e)"),
                                    ident[:, :]).then_inc(gate_t, 1)

            def hidden(s, par, e, loop=False):
                if e == 0:
                    pe.wait_ge(post_d, at(POST, G * s + G - 1, "x_lo"))
                if loop or E * s + e >= 2:
                    pe.wait_ge(u_done, E * s + e - 1)
                p = bank_h[e % 2]
                nc.tensor.matmul(p[:, :], w1_lo[:, e, :], x_hi[:, par, :], start=True, stop=False)
                nc.tensor.matmul(p[:, :], w1_hi[:, e, :], x_lo[:, par, :], start=False, stop=False)
                nc.tensor.matmul(p[:, :], w1_hi[:, e, :], x_hi[:, par, :], start=False, stop=True).then_inc(h_ready, 1)

            def output(s, par, e, loop=False):
                pe.wait_ge(hs_done, E * s + e + 1)
                if e == 0 and (loop or s > 0):
                    pe.wait_ge(y_added, s)
                for b in range(G):
                    mm = nc.tensor.matmul(bank_y[:, D * b:D * b + D], hs[:, e % 2, T * b:T * b + T], w2s[:, e, :],
                                          start=(e == 0 and b == 0), stop=(e == E - 1), skip_group_check=True)
                mm.then_inc(y_done, 1)

            pe.wait_ge(const_made, CONSTS)
            pe.wait_ge(w_made, WEIGHTS)

            def step(i, par, loop=False):
                nxt, more = i + 1, loop or i + 1 < S
                now = loop or i >= 0
                for j in range(SLOTS):
                    sf, d, (e0, e1) = ffn_units(i, j)
                    pf = par ^ d
                    ffn = exists(sf, loop)
                    ps_, pj = previous(i, j)
                    post = exists(ps_, loop) and now
                    pp = par if j else 1 - par
                    if now:
                        scoresT(i, par, j, 0, loop)
                        scoresT(i, par, j, 1, loop)
                    if ffn:
                        hidden(sf, pf, e0, loop)
                    if more and j == 0:
                        transposes(nxt, loop)
                    if post:
                        turn(G * ps_ + pj, pp, pj)
                    if now:
                        scoresT(i, par, j, 2, loop)
                    if ffn:
                        hidden(sf, pf, e1, loop)
                    if post:
                        route(G * ps_ + pj, pp, pj)
                    if now:
                        scoresT(i, par, j, 3, loop)
                    if ffn:
                        output(sf, pf, e0, loop)
                    if j == 0 and post:
                        gates_turn(i - 1)
                        pe.wait_ge(gate_d, at(GATE, i - 1, "gT"))
                    if now:
                        values(i, par, j, 0, loop)
                    if more and j == 0:
                        project(nxt, loop)
                    if now:
                        values(i, par, j, 1, loop)
                    if more and j >= 2:
                        for c in range(3):
                            scores(nxt, 1 - par, 2 * j - 4, c, loop)
                        max_turn(nxt, 2 * j - 4, loop)
                    if ffn:
                        output(sf, pf, e1, loop)
                    if now:
                        values(i, par, j, 2, loop)
                    if more and j >= 2:
                        for c in range(3):
                            scores(nxt, 1 - par, 2 * j - 3, c, loop)
                        max_turn(nxt, 2 * j - 3, loop)
                    if now:
                        values(i, par, j, 3, loop)

            def tail():
                n = G * (S - 1) + G - 1
                turn(n, 1, G - 1)
                route(n, 1, G - 1)
                gates_turn(S - 1)
                for e in range(E - 2, E):
                    hidden(S - 2, 0, e)
                    output(S - 2, 0, e)
                for e in range(E):
                    hidden(S - 1, 1, e)
                    if e:
                        output(S - 1, 1, e - 1)
                output(S - 1, 1, E - 1)

            steps(pe, step, tail)

        @block.scalar
        def _(act):
            def evacuate_xT(s):
                bank, n = ab(s, "xT")
                act.wait_ge(ab_ready[bank], n)
                nc.scalar.activation(xnT[:, :], bank_ab[bank][:, :], ACT.Identity, bias=col(NB_),
                                     scale=col(NG)).then_inc(ab_taken[bank], 1)

            def evacuate_kv(s, loop=False):
                bank, n = ab(s, "k")
                act.wait_ge(ab_ready[bank], n)
                if loop or s > 0:
                    act.wait_ge(split_k, at(SPLIT_QK, s - 1, "rest"))
                nc.scalar.activation(k32[:, :], bank_ab[bank][:, 0:G * N], ACT.Identity,
                                     bias=col(BK)).then_inc(ab_taken[bank], 1)
                for half_ in range(2):
                    bank, n = ab(s, f"v{half_}")
                    act.wait_ge(ab_ready[bank], n)
                    if half_ == 0 and (loop or s > 0):
                        act.wait_ge(split_v, at(SPLIT_V, s - 1, "rest"))
                    nc.scalar.activation(v32[:, 2 * half_:2 * half_ + 2, :].rearrange("n b d -> n (b d)"),
                                         bank_ab[bank][0:N, 0:2 * D], ACT.Copy,
                                         scale=col(GX, N)).then_inc(ab_taken[bank], 1)

            def evacuate_q(s, loop=False):
                bank, n = ab(s, "q")
                act.wait_ge(ab_ready[bank], n)
                if loop or s > 0:
                    act.wait_ge(split_q, at(SPLIT_QK, s - 1, "rest"))
                nc.scalar.activation(q32[:, :], bank_ab[bank][:, :], ACT.Identity,
                                     bias=col(BQS)).then_inc(ab_taken[bank], 1)

            def exponent(s, j, c, loop=False):
                m = NC * (G * s + j) + c
                act.wait_ge(s2_ready, m + 1)
                if loop or m >= LR:
                    act.wait_ge(pv_done, m - LR + 1)
                src = bank_s2[c % 2][0:N, :]
                nc.scalar.activation(p_hi[:, c, :], src, ACT.Exp).then_inc(hi_done, 1)
                nc.scalar.activation(p32[:, c, :], src, ACT.Exp).then_inc(p_done, 1)

            def square(s, e, loop=False):
                n = E * s + e
                act.wait_ge(u_done, n + 1)
                if loop or n >= 2:
                    act.wait_ge(y_done, n - 1)
                nc.scalar.activation(hs[:, e % 2, :], u[:, e % 2, :], ACT.Square).then_inc(hs_done, 1)

            def gate_exp(s):
                act.wait_ge(gate_d, at(GATE, s, "diff"))
                nc.scalar.activation(gt[:, 1, :], gt[:, 0, :], ACT.Exp).then_inc(gate_e, 1)

            act.wait_ge(w_in, 16 * 15)
            nc.scalar.activation(vec[:, GX:GX + 2], vec[:, GX:GX + 2], ACT.Tanh).then_inc(tanh_done, 1)
            act.wait_ge(tanh_done, 1)
            act.wait_ge(w_made, ONES + 1)

            def step(i, par, loop=False):
                nxt, more = i + 1, loop or i + 1 < S
                now = loop or i >= 0
                for j in range(SLOTS):
                    sf, d, (e0, e1) = ffn_units(i, j)
                    ffn = exists(sf, loop)
                    if now:
                        exponent(i, j, 0, loop)
                    if more and j == 0:
                        evacuate_xT(nxt)
                    if now:
                        exponent(i, j, 1, loop)
                    if ffn:
                        square(sf, e0, loop)
                    if now:
                        exponent(i, j, 2, loop)
                    if ffn:
                        square(sf, e1, loop)
                    if j == 0 and (loop or i > 0):
                        gate_exp(i - 1)
                    if now:
                        exponent(i, j, 3, loop)
                    if more and j == 0:
                        evacuate_kv(nxt, loop)
                        evacuate_q(nxt, loop)

            def tail():
                gate_exp(S - 1)
                for e in range(E - 2, E):
                    square(S - 2, e)
                for e in range(E):
                    square(S - 1, e)

            steps(act, step, tail)

        @block.vector
        def _(dve):
            def stats(s, par, loop=False):
                dve.wait_ge(ctx_in[par], landed(s, par))
                for b in range(G):
                    ins = nc.vector.bn_stats(c_st[:, b, :], ctx_sb[:, par, b, :])
                ins.then_inc(norm_d, 1)
                dve.wait_ge(x_in[par], landed(s, par))
                for b in range(G):
                    ins = nc.vector.bn_stats(x_st[:, b, :], x_sb[:, par, b, :])
                ins.then_inc(norm_d, 1)
                dve.wait_ge(norm_d, at(NORM, s, "ctx_stats"))
                apart(dve)
                for b in range(G):
                    ins = nc.vector.bn_aggr(c_mv[:, b, :], c_st[:, b, :])
                ins.then_inc(norm_d, 1)
                dve.wait_ge(norm_d, at(NORM, s, "x_stats"))
                apart(dve)
                for b in range(G):
                    ins = nc.vector.bn_aggr(x_mv[:, b, :], x_st[:, b, :])
                ins.then_inc(norm_d, 1)

            def normalise(s, par):
                dve.wait_ge(norm_p, at(NORM_P, s, "crstd"))
                for b in range(G):
                    ins = nc.vector.tensor_scalar(cn[:, b, :], ctx_sb[:, par, b, :], c_mv[:, b, 0:1],
                                                  nrm[0:N, 7, b:b + 1], ALU.subtract, ALU.mult)
                ins.then_inc(norm_d, 1)
                for b in range(G):
                    ins = nc.vector.tensor_scalar(xn[:, b, :], x_sb[:, par, b, :], x_mv[:, b, 0:1],
                                                  nrm[:, 5, b:b + 1], ALU.subtract, ALU.mult)
                ins.then_inc(norm_d, 1)

            def evacuate_ctxT(s):
                bank, n = ab(s, "ctxT")
                dve.wait_ge(ab_ready[bank], n)
                nc.vector.tensor_scalar(cnT[0:L, :], bank_ab[bank][0:L, 0:G * N], col(TG, L), col(TB, L),
                                        ALU.mult, ALU.add).then_inc(ab_taken[bank], 1)

            def split(s, name, done, src, rest, parts, loop=False, last=None):
                if last is not None:
                    bank, n = ab(s, last)
                    dve.wait_ge(ab_taken[bank], n)
                nc.vector.tensor_copy(parts[0], src).then_inc(done, 1)
                dve.wait_ge(done, at(SPLIT_QK, s, "hi"))
                nc.vector.tensor_tensor(rest, src, parts[0], ALU.subtract).then_inc(done, 1)
                dve.wait_ge(done, at(SPLIT_QK, s, "rest"))
                nc.vector.tensor_copy(parts[1], rest).then_inc(done, 1)
                dve.wait_ge(done, at(SPLIT_QK, s, "mid"))
                nc.vector.tensor_tensor(parts[2], rest, parts[1], ALU.subtract).then_inc(done, 1)

            def split_keys(s, par, loop=False):
                if loop or s > 0:
                    dve.wait_ge(k_stacked[1 - par], landed(s - 1, 1 - par, TERMS))
                split(s, "k", split_k, k32[:, :], k_rest[:, :], [k_parts[:, a, :] for a in range(PARTS)], last="k")

            def split_queries(s, par, loop=False):
                if loop or s > 0:
                    dve.wait_ge(q_stacked[1 - par], landed(s - 1, 1 - par, TERMS))
                split(s, "q", split_q, q32[:, :], q_rest[:, :], [q_parts[:, a, :] for a in range(PARTS)], last="q")

            def split_values(s, par, loop=False):
                if loop or s >= 2:
                    dve.wait_ge(pv_done, NC * G * (s - 1))
                bank, n = ab(s, "v0")
                dve.wait_ge(ab_taken[bank], n)
                view = vs[:, par, :, :, 0:HD * PARTS].rearrange("n b h (d a) -> n a (b h) d", a=PARTS)
                split(s, "v", split_v, v32[:, :, :].rearrange("n b (h d) -> n (b h) d", d=HD),
                      v_rest[:, :, :].rearrange("n b (h d) -> n (b h) d", d=HD),
                      [view[:, a] for a in range(PARTS)], last="v1")

            def maximum(s, j, c, loop=False):
                n = G * s + j
                h0, h1 = HEADS_S1[c]
                bank, k = ab(s, f"s1{'abc'[c]}{j}")
                dve.wait_ge(ab_ready[bank], k)
                nc.vector.tensor_reduce(negm[:, h0:h1],
                                        bank_ab[bank][:, 0:N * (h1 - h0)].rearrange("t (h n) -> t h n", n=N),
                                        AX.X, ALU.max, negate=True).then_inc(ab_taken[bank], 1)

            def max_parts(s, j, loop=False):
                n = G * s + j
                for c in range(3):
                    bank, k = ab(s, f"s1{'abc'[c]}{j}")
                    dve.wait_ge(ab_taken[bank], k)
                nc.vector.tensor_copy(m_parts[:, 0, :], negm[:, :]).then_inc(max_d, 1)
                dve.wait_ge(max_d, at(MAXP, n, "hi"))
                nc.vector.tensor_tensor(m_rest[:, :], negm[:, :], m_parts[:, 0, :], ALU.subtract).then_inc(max_d, 1)
                dve.wait_ge(max_d, at(MAXP, n, "rest"))
                nc.vector.tensor_copy(m_parts[:, 1, :], m_rest[:, :]).then_inc(max_d, 1)
                dve.wait_ge(max_d, at(MAXP, n, "mid"))
                nc.vector.tensor_tensor(m_parts[:, 2, :], m_rest[:, :], m_parts[:, 1, :],
                                        ALU.subtract).then_inc(max_d, 1)

            def max_store(s, j, loop=False):
                bank, k = ab(s, f"mT{j}")
                dve.wait_ge(ab_ready[bank], k)
                if j >= 2:
                    dve.wait_ge(m_in[j - 2], 16 * s + 16)
                elif loop or s > 0:
                    dve.wait_ge(m_in[j + 2], 16 * s)
                nc.vector.tensor_copy(mT[:, j % 2, :], bank_ab[bank][:, :].bitcast(BF16)[0:PARTS * H, 0:T])\
                    .then_inc(ab_taken[bank], 1)

            def attended(n, s, par, j, loop=False):
                dve.wait_ge(pv_done, NC * n + NC)
                view = bank_c[:, 0:VC * H].rearrange("t (h v) -> t h v", v=VC)
                nc.vector.tensor_reduce(o[:, :].rearrange("t (h d) -> t h d", d=HD),
                                        view[:, :, 0:HD * PARTS].rearrange("t h (d a) -> t h d a", a=PARTS),
                                        AX.X, ALU.add).then_inc(post_d, 1)
                nc.vector.reciprocal(rden[:, :].rearrange("t (h o) -> t h o", o=1),
                                     view[:, :, HD * PARTS:VC]).then_inc(post_d, 1)
                dve.wait_ge(post_d, at(POST, n, "recip"))
                nc.vector.tensor_tensor(o[:, :].rearrange("t (h d) -> t h d", d=HD),
                                        o[:, :].rearrange("t (h d) -> t h d", d=HD),
                                        rden[:, :].rearrange("t (h o) -> t h o", o=1).broadcast_to([T, H, HD]),
                                        ALU.mult).then_inc(post_d, 1)
                if j == 0:
                    dve.wait_ge(res_in[par], landed(s, par))
                dve.wait_ge(post_d, at(POST, n, "scaled"))
                nc.vector.tensor_tensor(x1[:, par, j, :], x_res[:, par, j, :], o[:, :], ALU.add).then_inc(post_d, 1)
                dve.wait_ge(post_d, at(POST, n, "x1"))
                nc.vector.bn_stats(st2[:, :], x1[:, par, j, :]).then_inc(post_d, 1)
                dve.wait_ge(post_d, at(POST, n, "stats"))
                apart(dve)
                nc.vector.bn_aggr(mv2[:, :], st2[:, :]).then_inc(post_d, 1)

            def normalise2(n, par, j):
                dve.wait_ge(post_p, at(POST_P, n, "rstd"))
                nc.vector.tensor_scalar(xn2[:, :], x1[:, par, j, :], mv2[:, 0:1], rs2[:, 1:2], ALU.subtract,
                                        ALU.mult).then_inc(post_d, 1)

            def turned(n, s, par, j):
                dve.wait_ge(post_t, n + 1)
                nc.vector.tensor_copy(xT32[:, j % 2, :], bank_c[:, 0:T]).then_inc(post_d, 1)
                dve.wait_ge(post_d, at(POST, n, "xT"))
                hi = x_hi[:, par, T * j:T * j + T]
                nc.vector.tensor_copy(hi, xT32[:, j % 2, :]).then_inc(post_d, 1)
                dve.wait_ge(post_d, at(POST, n, "x_hi"))
                nc.vector.tensor_tensor(x_lo[:, par, T * j:T * j + T], xT32[:, j % 2, :], hi.bitcast(F32),
                                        ALU.subtract).then_inc(post_d, 1)

            def routed(n, j):
                dve.wait_ge(post_l, n + 1)
                nc.vector.tensor_copy(logits[:, j, :], bank_c[:, 256:256 + E]).then_inc(post_d, 1)
                dve.wait_ge(post_d, at(POST, n, "logits"))
                apart(dve)
                nc.vector.max(top[:, j, :], logits[:, j, :]).then_inc(post_d, 1)
                dve.wait_ge(post_d, at(POST, n, "top"))
                apart(dve)
                nc.vector.max_index(index[:, j, :], top[:, j, :], logits[:, j, :]).then_inc(post_d, 1)

            def gate(s):
                dve.wait_ge(post_d, at(POST, G * s + G - 1, "index"))
                nc.vector.tensor_tensor(gt[:, 0, :], top[:, :, 1], top[:, :, 0], ALU.subtract).then_inc(gate_d, 1)
                dve.wait_ge(gate_e, s + 1)
                nc.vector.tensor_scalar(gt[:, 2, :], gt[:, 1, :], 1.0, None, ALU.add).then_inc(gate_d, 1)
                dve.wait_ge(gate_d, at(GATE, s, "den"))
                nc.vector.reciprocal(gt[:, 3, :], gt[:, 2, :]).then_inc(gate_d, 1)
                dve.wait_ge(gate_d, at(GATE, s, "p1"))
                nc.vector.tensor_tensor(gt[:, 4, :], gt[:, 1, :], gt[:, 3, :], ALU.mult).then_inc(gate_d, 1)
                nc.vector.tensor_copy(idx_f[:, :, :], index[:, :, 0:2]).then_inc(gate_d, 1)
                dve.wait_ge(gate_d, at(GATE, s, "idx_f"))
                for which, dst in ((0, eq1), (1, eq2)):
                    nc.vector.tensor_tensor(dst[:, :, :], iota[:, :, :],
                                            idx_f[:, :, which:which + 1].broadcast_to([T, G, E]),
                                            ALU.is_equal).then_inc(gate_d, 1)
                dve.wait_ge(gate_p, s + 1)
                dve.wait_ge(gate_d, at(GATE, s, "eq2"))
                for which, dst in ((0, eq1), (1, eq2)):
                    sq = gate_s[:, which, :].rearrange("t (b o) -> t b o", o=1)
                    nc.vector.tensor_tensor(dst[:, :, :], dst[:, :, :], sq.broadcast_to([T, G, E]),
                                            ALU.mult).then_inc(gate_d, 1)
                dve.wait_ge(gate_d, at(GATE, s, "g2"))
                nc.vector.tensor_tensor(gates[:, :, :], eq1[:, :, :], eq2[:, :, :], ALU.add).then_inc(gate_d, 1)

            def gate_rows(s, par, loop=False):
                dve.wait_ge(gate_t, s + 1)
                nc.vector.tensor_copy(gatesT[:, :], bank_c[0:G * E, 0:T]).then_inc(gate_d, 1)

            def gated(s, par, e, loop=False):
                n = E * s + e
                if e == 0:
                    dve.wait_ge(g_in[par], landed(s, par, 2))
                dve.wait_ge(h_ready, n + 1)
                if loop or n >= 2:
                    dve.wait_ge(hs_done, n - 1)
                nc.vector.scalar_tensor_tensor(out=u[:, e % 2, :], in0=bank_h[e % 2][:, :], scalar=0.0,
                                               in1=gb[:, par, e, :], op0=ALU.max, op1=ALU.mult).then_inc(u_done, 1)

            def finish(s, par, loop=False):
                dve.wait_ge(y_done, E * s + E)
                dve.wait_ge(stored[par], landed(s, par))
                nc.vector.tensor_tensor(y_out[:, par].rearrange("t b d -> t (b d)"),
                                        x1[:, par].rearrange("t b d -> t (b d)"), bank_y[:, :],
                                        ALU.add).then_inc(y_added, 1)

            nc.vector.memset(ks[64:MR, :, :, :], 1.0).then_inc(w_made, 1)
            nc.vector.memset(cnT[L:L + 1, :], 1.0).then_inc(w_made, 1)
            nc.vector.memset(vs[:, :, :, :, :], 1.0).then_inc(w_made, 1)
            dve.wait_ge(w_in, 16 * 15)
            dve.wait_ge(const_made, CONSTS)
            nc.vector.tensor_scalar(col(BQS), col(BQ), SCALE, None, ALU.mult).then_inc(w_made, 1)
            nc.vector.tensor_scalar(wq[:, :].rearrange("c (d h) -> c d h", d=HD),
                                    wq_in[:, :].rearrange("c (h d) -> c d h", d=HD), SCALE, None,
                                    ALU.mult).then_inc(w_made, 1)
            nc.vector.tensor_copy(wk[:, :].rearrange("c (d h) -> c d h", d=HD),
                                  wk_in[:, :].rearrange("c (h d) -> c d h", d=HD)).then_inc(w_made, 1)
            nc.vector.tensor_copy(ident_bf[:, :], ident[:, :]).then_inc(w_made, 1)
            nc.vector.tensor_copy(w1_hi[:, :, :], w1_in[:, :, :]).then_inc(w_made, 1)
            dve.wait_ge(w_made, ONES + 5)
            nc.vector.tensor_tensor(w1_lo[:, :, :], w1_in[:, :, :], w1_hi[:, :, :].bitcast(F32),
                                    ALU.subtract).then_inc(w_made, 1)
            dve.wait_ge(tanh_done, 1)
            nc.vector.tensor_scalar(w2s[:, :, :], w2_in[:, :, :], col(GF), None, ALU.mult).then_inc(w_made, 1)
            dve.wait_ge(w_made, WEIGHTS)

            def step(i, par, loop=False):
                nxt, more = i + 1, loop or i + 1 < S
                now = loop or i >= 0
                for j in range(SLOTS):
                    sf, d, (e0, e1) = ffn_units(i, j)
                    pf = par ^ d
                    ffn = exists(sf, loop)
                    ps_, pj = previous(i, j)
                    post = exists(ps_, loop) and now
                    pp = par if j else 1 - par
                    n = G * ps_ + pj
                    if post:
                        attended(n, ps_, pp, pj, loop)
                    if more and j == 0:
                        stats(nxt, 1 - par, loop)
                    if ffn:
                        gated(sf, pf, e0, loop)
                    if post:
                        normalise2(n, pp, pj)
                    if more and j == 0:
                        normalise(nxt, 1 - par)
                        evacuate_ctxT(nxt)
                    if post:
                        turned(n, ps_, pp, pj)
                    if ffn:
                        gated(sf, pf, e1, loop)
                    if post:
                        routed(n, pj)
                    if j == 0 and post:
                        gate(i - 1)
                        gate_rows(i - 1, 1 - par, loop)
                    if more and j == 0:
                        split_keys(nxt, 1 - par, loop)
                        split_values(nxt, 1 - par, loop)
                        split_queries(nxt, 1 - par, loop)
                    if j == 0 and ffn:
                        finish(sf, pf, loop)
                    if more and j >= 2:
                        for jj in (2 * j - 4, 2 * j - 3):
                            for c in range(3):
                                maximum(nxt, jj, c, loop)
                            max_parts(nxt, jj, loop)
                            max_store(nxt, jj, loop)

            def tail():
                n = G * (S - 1) + G - 1
                attended(n, S - 1, 1, G - 1)
                normalise2(n, 1, G - 1)
                turned(n, S - 1, 1, G - 1)
                routed(n, G - 1)
                gate(S - 1)
                gate_rows(S - 1, 1)
                for e in range(E - 2, E):
                    gated(S - 2, 0, e)
                finish(S - 2, 0)
                for e in range(E):
                    gated(S - 1, 1, e)
                finish(S - 1, 1)

            steps(dve, step, tail)

        @block.gpsimd
        def _(pool):
            def norm_rstd(s):
                pool.wait_ge(norm_d, at(NORM, s, "x_moments"))
                apart(pool)
                var, cvar = x_mv[:, :, 1], c_mv[:, :, 1]
                nc.gpsimd.tensor_scalar(nrm[:, 0, :], var, EPS, None, ALU.add).then_inc(norm_p, 1)
                pool.wait_ge(norm_p, at(NORM_P, s, "var_eps"))
                nc.gpsimd.tensor_tensor(nrm[:, 1, :], nrm[:, 0, :], neg_half[:, :], ALU.pow).then_inc(norm_p, 1)
                pool.wait_ge(norm_p, at(NORM_P, s, "rstd1"))
                nc.gpsimd.tensor_tensor(nrm[:, 2, :], var, nrm[:, 1, :], ALU.mult).then_inc(norm_p, 1)
                pool.wait_ge(norm_p, at(NORM_P, s, "v_r"))
                nc.gpsimd.tensor_tensor(nrm[:, 3, :], nrm[:, 2, :], nrm[:, 1, :], ALU.mult).then_inc(norm_p, 1)
                pool.wait_ge(norm_p, at(NORM_P, s, "v_rr"))
                apart(pool)
                nc.gpsimd.tensor_scalar(nrm[:, 4, :], nrm[:, 3, :], EPS, None, ALU.add).then_inc(norm_p, 1)
                pool.wait_ge(norm_p, at(NORM_P, s, "v2_eps"))
                nc.gpsimd.tensor_tensor(nrm[:, 0, :], nrm[:, 4, :], neg_half[:, :], ALU.pow).then_inc(norm_p, 1)
                pool.wait_ge(norm_p, at(NORM_P, s, "rstd2"))
                nc.gpsimd.tensor_tensor(nrm[:, 5, :], nrm[:, 0, :], nrm[:, 1, :], ALU.mult).then_inc(norm_p, 1)
                nc.gpsimd.tensor_scalar(nrm[0:N, 6, :], cvar, EPS, None, ALU.add).then_inc(norm_p, 1)
                pool.wait_ge(norm_p, at(NORM_P, s, "cvar_eps"))
                nc.gpsimd.tensor_tensor(nrm[0:N, 7, :], nrm[0:N, 6, :], neg_half[0:N, :],
                                        ALU.pow).then_inc(norm_p, 1)

            def low_part(s, j, c):
                m = NC * (G * s + j) + c
                pool.wait_ge(hi_done, m + 1)
                pool.wait_ge(p_done, m + 1)
                nc.gpsimd.tensor_tensor(p_lo[:, c, :], p32[:, c, :], p_hi[:, c, :],
                                        ALU.subtract).then_inc(lo_done, 1)

            def rstd(n):
                pool.wait_ge(post_d, at(POST, n, "moments"))
                apart(pool)
                nc.gpsimd.tensor_scalar(rs2[:, 0:1], mv2[:, 1:2], EPS, None, ALU.add).then_inc(post_p, 1)
                pool.wait_ge(post_p, at(POST_P, n, "var_eps"))
                nc.gpsimd.tensor_tensor(rs2[:, 1:2], rs2[:, 0:1], neg_half[:, 0:1], ALU.pow).then_inc(post_p, 1)

            def gate_roots(s):
                pool.wait_ge(gate_d, at(GATE, s, "p2"))
                nc.gpsimd.tensor_tensor(gate_s[:, :, :].rearrange("t a b -> t (a b)"),
                                        gt[:, 3:5, :].rearrange("t a b -> t (a b)"), half[:, :],
                                        ALU.pow).then_inc(gate_p, 1)

            nc.gpsimd.memset(ident[:, :], 0.0).then_inc(const_made, 1)
            pool.wait_ge(const_made, 1)
            nc.gpsimd.affine_select(out=ident[:, :], in_=ident[:, :], compare_op=ALU.not_equal, fill=1.0, base=0,
                                    pattern=[[-1, 128]], channel_multiplier=1).then_inc(const_made, 1)
            nc.gpsimd.memset(half[:, :], 0.5).then_inc(const_made, 1)
            nc.gpsimd.memset(neg_half[:, :], -0.5).then_inc(const_made, 1)
            for e in range(E):
                nc.gpsimd.memset(iota[:, :, e], float(e)).then_inc(const_made, 1)
            for par in range(2):
                nc.gpsimd.memset(y_out[:, par, :, :], 0.0).then_inc(stored[par], 16)

            def step(i, par, loop=False):
                nxt, more = i + 1, loop or i + 1 < S
                now = loop or i >= 0
                for j in range(SLOTS):
                    ps_, pj = previous(i, j)
                    post = exists(ps_, loop) and now
                    if now:
                        low_part(i, j, 0)
                    if post:
                        rstd(G * ps_ + pj)
                    if more and j == 0:
                        norm_rstd(nxt)
                    if now:
                        low_part(i, j, 1)
                        low_part(i, j, 2)
                    if j == 0 and post:
                        gate_roots(i - 1)
                    if now:
                        low_part(i, j, 3)

            def tail():
                rstd(G * (S - 1) + G - 1)
                gate_roots(S - 1)

            steps(pool, step, tail)


_INS = ["x", "ctx_768", "g_xattn", "g_ffn", "L0_xattn_norm_g", "L0_xattn_norm_b", "L0_xattn_tnorm_g",
        "L0_xattn_tnorm_b", "L0_xattn_Wq", "L0_xattn_bq", "L0_xattn_Wk", "L0_xattn_bk", "L0_xattn_Wv",
        "L0_xattn_bv", "L0_ffn_w_router", "L0_ffn_w1", "L0_ffn_w2"]


def kernel(**inputs):
    import numpy as _np
    import concourse.bacc as _bacc
    from concourse import mybir as _mybir
    from concourse.bass_utils import run_bass_kernel_spmd as _run

    nc = _bacc.Bacc("TRN2", target_bir_lowering=False, num_devices=1)
    arrays, args = {}, []
    for name in _INS:
        a = _np.ascontiguousarray(inputs[name])
        arrays[f"in_{name}_dram"] = a
        args.append(nc.dram_tensor(f"in_{name}_dram", a.shape, _mybir.dt.from_np(a.dtype), kind="ExternalInput").ap())
    args.append(nc.dram_tensor("out_0_dram", tuple(inputs["x"].shape), _mybir.dt.float32, kind="ExternalOutput").ap())
    flamingo_kernel(nc, *args)
    r = _run(nc, [arrays], core_ids=[0])
    return r.results[0]["out_0_dram"]
```

```python
from contextlib import ExitStack

import concourse.bass as bass
from concourse import mybir

ALU = mybir.AluOpType
ACT = mybir.ActivationFunctionType
AX = mybir.AxisListType
F32 = mybir.dt.float32
F32R = mybir.dt.float32r
BF16 = mybir.dt.bfloat16
F16 = mybir.dt.float16
U32 = mybir.dt.uint32

G = 4
PARTS = 3
TERMS = PARTS * PARTS
HEADS_S1 = [(0, 6), (6, 12), (12, 16)]
CH = 4
SLOTS = 4
EPS = 1e-5


def landed(s, par, dmas=1):
    return dmas * (8 * (s - par) + 16)


def at(steps, n, name):
    return len(steps) * n + steps.index(name) + 1


AB_USES = [
    (-1, "turn2"), (0, "s1c2"), (-1, "route2"), (1, "k"), (0, "mT2"), (1, "q"), (0, "s1a3"), (0, "s1b3"),
    (-1, "turn3"), (0, "s1c3"), (-1, "route3"), (1, "v"), (0, "mT3"), (-1, "gates"), (1, "s1a0"), (1, "s1b0"),
    (0, "turn0"), (1, "s1c0"), (0, "route0"), (1, "mT0"), (1, "s1a1"), (1, "s1b1"),
    (0, "turn1"), (1, "s1c1"), (0, "route1"), (1, "mT1"), (2, "ctxT"), (1, "s1a2"), (1, "s1b2"), (2, "xT"),
]
AB_SHIFT = {name: -shift for shift, name in AB_USES}
AB_HALF = len(AB_USES) // 2


def ab_order(step, tiles):
    return [name for shift, name in AB_USES if 0 <= step + shift < tiles]


STATS = ["ctx_stats", "x_stats", "ctx_moments", "x_moments"]
NORM = ["ctx_normed", "x_normed"]
NORM_P = ["cvar_eps", "crstd", "var_eps", "rstd"]
SPLIT = ["rest", "mid", "lo"]
MAXP = ["hi", "rest", "mid", "lo"]
POST = ["summed", "recip", "scaled", "x1", "stats", "moments", "normed"]
LATE = ["top", "x_lo"]
POST_P = ["var_eps", "rstd"]
GATE = ["diff", "index", "den", "idx_f", "eq1", "eq2", "second", "both", "gates"]


def flamingo_kernel(nc, x, ctx, g_xattn, g_ffn, norm_g, norm_b, tnorm_g, tnorm_b,
                    Wq, bq, Wk, bk, Wv, bv, w_router, w1, w2, out):
    B, T, D = x.shape
    N, L = ctx.shape[1:]
    E = w_router.shape[1]
    H = 16
    HD = D // H
    S = B // G
    GT = G * T
    QR = TERMS * HD
    Q_DMAS = 2 * PARTS - 1
    MR = QR + PARTS
    NC = H // CH
    VC = HD * PARTS + 1
    SCALE = float(HD) ** -0.5
    GATE_CUTS = (0, 2, 5, E)
    assert T == 128 and D == 128 and S % 2 == 0 and S >= 6 and E == 8

    x_v = x.rearrange("(s g) t d -> s t g d", g=G)
    ctx_v = ctx.rearrange("(s g) n l -> s n g l", g=G)
    out_v = out.rearrange("(s g) t d -> s t g d", g=G)
    gates_dram = nc.dram_tensor("gates_scratch", [2, E, G, T], F32, kind="Internal").ap()

    with ExitStack() as stack:
        def sb(name, shape, dt=F32):
            return stack.enter_context(nc.sbuf_tensor(name, shape, dt))

        def sem(name):
            return stack.enter_context(nc.semaphore(name))

        def sems(name, n):
            return [sem(f"{name}{i}") for i in range(n)]

        ident = sb("ident", [128, 128])
        ident_bf = sb("ident_bf", [128, 128], BF16)
        ones = sb("ones", [PARTS, G * N], BF16)
        neg_half = sb("neg_half", [128, G])
        iota = sb("iota", [128, G, E])
        wq_in = sb("wq_in", [D, D])
        wk_in = sb("wk_in", [L, D])
        wq = sb("wq", [D, D])
        wk = sb("wk", [L, D])
        wv = sb("wv", [L + 1, D])
        wr = sb("wr", [D, E])
        w1_in = sb("w1_in", [D, E, D])
        w2_in = sb("w2_in", [D, E, D])
        w1_hi = sb("w1_hi", [D, E, D], F32R)
        w1_lo = sb("w1_lo", [D, E, D], F32R)
        w2s = sb("w2s", [D, E, D])
        vec = sb("vec", [128, 10])
        CONSTS, ONES, WEIGHTS = 11, 3, 4
        HW_WEIGHTS, POOL_WEIGHTS = 9, 3
        NG, NB_, BQ, BK, TG, TB, GX, GF, BQS = range(9)

        def col(i, n=128):
            return vec[0:n, i:i + 1]

        x_sb = sb("x_sb", [T, 2, G, D])
        ctx_sb = sb("ctx_sb", [N, 2, G, L])
        x_res = sb("x_res", [T, 2, G, D])
        x_st = sb("x_st", [T, G, 6])
        c_st = sb("c_st", [N, G, 6])
        x_mv = sb("x_mv", [T, G, 2])
        c_mv = sb("c_mv", [N, G, 2])
        nrm = sb("nrm", [T, 4, G])
        xn = sb("xn", [T, G, D])
        cn = sb("cn", [N, G, L])
        xnT = sb("xnT", [D, GT])
        cnT = sb("cnT", [L + 1, G * N])
        q32 = sb("q32", [D, GT])
        k32 = sb("k32", [D, G * N])
        v32 = sb("v32", [N, G, D])
        q_rest = sb("q_rest", [D, GT])
        k_rest = sb("k_rest", [D, G * N])
        v_rest = sb("v_rest", [N, G, D])
        q_parts = sb("q_parts", [D, PARTS, GT], BF16)
        k_parts = sb("k_parts", [D, PARTS, G * N], BF16)
        qs = sb("qs", [MR, 2, H, GT], BF16)
        ks = sb("ks", [MR, 2, H, G * N], BF16)
        vs = sb("vs", [N, 2, G, H, VC], BF16)
        negm = sb("negm", [T, H])
        m_rest = sb("m_rest", [T, H])
        m_parts = sb("m_parts", [T, PARTS, H], BF16)
        mT = sb("mT", [PARTS * H, 2, T], BF16)
        LR = NC
        p32 = sb("p32", [N, LR, CH * T])
        p_hi = sb("p_hi", [N, LR, CH * T], F16)
        p_lo = sb("p_lo", [N, LR, CH * T], F16)
        o = sb("o", [T, D])
        rden = sb("rden", [T, H])
        x1 = sb("x1", [T, 2, G, D])
        st2 = sb("st2", [T, 6])
        mv2 = sb("mv2", [T, 2])
        rs2 = sb("rs2", [T, 2])
        xn2 = sb("xn2", [T, D])
        xT32 = sb("xT32", [D, 2, T])
        x_hi = sb("x_hi", [D, 2, GT], F32R)
        x_lo = sb("x_lo", [D, 2, GT], F32R)
        logits = sb("logits", [T, G, E])
        top = sb("top", [T, G, E])
        index = sb("index", [T, G, E], U32)
        gt = sb("gt", [T, 8, G])
        idx_f = sb("idx_f", [T, G, 2])
        eq1 = sb("eq1", [T, G, E])
        eq2 = sb("eq2", [T, G, E])
        gates = sb("gates", [T, E, G])
        gatesT = sb("gatesT", [G * E, T])
        gb = sb("gb", [D, 2, E, GT])
        u = sb("u", [D, 2, GT])
        hs = sb("hs", [D, 2, GT])
        y_out = sb("y_out", [T, 2, G, D])

        def ps(name):
            return stack.enter_context(nc.psum_tensor(name, [128, 512], F32))

        bank_s2 = [ps("s2_0"), ps("s2_1")]
        bank_h = [ps("h_0"), ps("h_1")]
        bank_y = ps("y")
        bank_c = ps("c")
        bank_ab = [ps("ab_0"), ps("ab_1")]

        w_in, w_in_pool, experts_in = sem("w_in"), sem("w_in_pool"), sem("experts_in")
        const_made = sem("const_made")
        w_made, experts_made = sem("w_made"), sem("experts_made")
        tanh_done = sem("tanh_done")
        x_in, ctx_in, res_in = sems("x_in", 2), sems("ctx_in", 2), sems("res_in", 2)
        ab_ready, ab_taken = sems("ab_ready", 2), sems("ab_taken", 2)
        stats_d, norm_d, norm_p = sem("stats_d"), sem("norm_d"), sem("norm_p")
        split_q, split_k, split_v = sem("split_q"), sem("split_k"), sem("split_v")
        q_stacked, k_stacked = sems("q_stacked", 2), sems("k_stacked", 2)
        ones_made, ones_in = sem("ones_made"), sem("ones_in")
        max_d = sem("max_d")
        m_in = sems("m_in", G)
        s2_ready = sem("s2_ready")
        hi_done, p_done, lo_done = sem("hi_done"), sem("p_done"), sem("lo_done")
        pv_done = sem("pv_done")
        post_d, post_p, late_d = sem("post_d"), sem("post_p"), sem("late_d")
        gate_d, gate_e, gate_p = sem("gate_d"), sem("gate_e"), sem("gate_p")
        g_stored = sems("g_stored", 2)
        g_in = [sems(f"g_in{par}_", len(GATE_CUTS) - 1) for par in range(2)]
        xT_done, hi_k, hi_q = sem("xT_done"), sem("hi_k"), sem("hi_q")
        h_ready, u_done, hs_done, y_done = sem("h_ready"), sem("u_done"), sem("hs_done"), sem("y_done")
        y_added = sem("y_added")
        stored = sems("stored", 2)

        held_apart = sem("held_apart")

        block = stack.enter_context(nc.Block())

        def apart(eng):
            eng.sem_inc(held_apart, 1)

        def ab(s, name):
            step = s + AB_SHIFT[name]
            if isinstance(s, int):
                before = sum(len(ab_order(t, S)) for t in range(-2, step))
                k = before + ab_order(step, S).index(name)
                return k % 2, k // 2 + 1
            k = sum(len(ab_order(t, S)) for t in (-2, -1, 0)) - len(AB_USES) + ab_order(1, S).index(name)
            return k % 2, AB_HALF * step + k // 2 + 1

        def steps(eng, step):
            step(-2, 0)
            step(-1, 1)
            step(0, 0)
            step(1, 1)
            with eng.Fori(1, S // 2 - 1) as pair:
                step(2 * pair, 0, loop=True)
                step(2 * pair + 1, 1, loop=True)
            for i in range(S - 2, S + 2):
                step(i, i % 2)

        def ffn_units(i, j):
            return ((i - 2, 0, 4, (5, 6, 7)), (i - 2, 0, 7, (None, None, None)),
                    (i - 1, 1, None, (None, 0, 1)), (i - 1, 1, 1, (2, 3, 4)))[j]

        def slots(i, par, loop=False):

            def batch(t, b):
                t, d, b = t + b // G, (b // G) % 2, b % G
                return (t, par ^ d, b) if exists(t, loop) else None

            for j in range(SLOTS):
                near = {k: batch(i, j + k) for k in range(-2, 4)}
                nxt = (i + 1, 1 - par) if exists(i + 1, loop) else None
                third = (i + 2, par) if exists(i + 2, loop) else None
                sf, d, pending, experts = ffn_units(i, j)
                ffn = (sf, par ^ d, pending, experts) if exists(sf, loop) else (sf, par ^ d, None, (None,) * 3)
                yield j, near, nxt, third, ffn

        def exists(t, loop=False):
            return loop or 0 <= t < S

        @block.sync
        def _(sp):
            def load(s, par, loop=False):
                if loop or s >= 2:
                    sp.wait_ge(norm_d, at(NORM, s - 2, "x_normed"))
                    apart(sp)
                sp.dma_start(ctx_sb[:, par], ctx_v[s]).then_inc(ctx_in[par], 16)
                sp.dma_start(x_sb[:, par], x_v[s]).then_inc(x_in[par], 16)

            def load_rows(s, par, loop=False):
                if loop or s >= 2:
                    sp.wait_ge(post_d, at(POST, G * (s - 2) + G - 1, "x1"))
                    apart(sp)
                sp.dma_start(x_res[:, par], x_v[s]).then_inc(res_in[par], 16)

            def stack_k(s, par, b, loop=False):
                if b == 0:
                    if loop or s >= 2:
                        sp.wait_ge(s2_ready, NC * G * (s - 1))
                        apart(sp)
                    sp.wait_ge(hi_k, s + 1)
                else:
                    sp.wait_ge(split_k, at(SPLIT, s, SPLIT[b]))
                for group in range(PARTS):
                    r = HD * (PARTS * group + (b - group) % PARTS)
                    sp.dma_start(ks[r:r + HD, par], k_parts[:, b, :]).then_inc(k_stacked[par], 16)

            def stack_q(s, par, a, loop=False):
                if a == 0:
                    sp.wait_ge(hi_q, s + 1)
                else:
                    sp.wait_ge(split_q, at(SPLIT, s, SPLIT[a]))
                sp.dma_start(qs[HD * a:HD * a + HD, par], q_parts[:, a, :]).then_inc(q_stacked[par], 16)

            def repeat_q(s, par):
                sp.wait_ge(q_stacked[par], landed(s, par, Q_DMAS) - 16 * (Q_DMAS - PARTS))
                for group in range(1, PARTS):
                    r = HD * PARTS * group
                    sp.dma_start(qs[r:r + HD * PARTS, par], qs[0:HD * PARTS, par]).then_inc(q_stacked[par], 16)

            def max_rows(s, par, j):
                bank, n = ab(s, f"mT{j}")
                sp.wait_ge(ab_taken[bank], n)
                sp.dma_start(qs[QR:MR, par, :, T * j:T * j + T], mT[:, j % 2, :]).then_inc(m_in[j], 16)

            def spread_gates(s, par):
                bank, n = ab(s, "gates")
                sp.wait_ge(ab_taken[bank], n)
                sp.dma_start(gates_dram[par].rearrange("e b t -> (e b) t"), gatesT[:, :]).then_inc(g_stored[par], 16)

            def broadcast_gates(s, par, part):
                if part == 0:
                    sp.wait_ge(g_stored[par], landed(s, par))
                e0, e1 = GATE_CUTS[part], GATE_CUTS[part + 1]
                src = gates_dram[par, e0:e1].rearrange("e b t -> (e b t)").rearrange("(o n) -> o n", o=1)
                sp.dma_start(gb[:, par, e0:e1].rearrange("p e n -> p (e n)"),
                             src.broadcast_to([D, (e1 - e0) * GT])).then_inc(g_in[par][part], 16)

            def store(s, par):
                sp.wait_ge(y_added, s + 1)
                apart(sp)
                sp.dma_start(out_v[s], y_out[:, par]).then_inc(stored[par], 16)

            load(0, 0)
            for dst, src in ((wk_in[:, :], Wk), (col(TG, L), tnorm_g.rearrange("(n o) -> n o", o=1)),
                             (col(TB, L), tnorm_b.rearrange("(n o) -> n o", o=1)),
                             (col(BK), bk.rearrange("(h d o) -> d h o", d=HD, o=1)),
                             (wq_in[:, :], Wq), (wv[0:L, :], Wv),
                             (wv[L:L + 1, :], bv.rearrange("(o n) -> o n", o=1))):
                with nc.allow_non_contiguous_dma(reason="short vectors"):
                    sp.dma_start(dst, src).then_inc(w_in, 16)
            sp.wait_ge(ones_made, 1)
            for par in range(2):
                sp.dma_start(ks[QR:MR, par], ones[:, :].rearrange("p (o n) -> p o n", o=1)
                             .broadcast_to([PARTS, H, G * N])).then_inc(ones_in, 16)

            def step(i, par, loop=False):
                for j, near, nxt, third, ffn in slots(i, par, loop):
                    if j == 0 and nxt:
                        stack_k(i + 1, 1 - par, 0, loop)
                    if near[2]:
                        max_rows(*near[2])
                    if j == 0 and nxt:
                        stack_k(i + 1, 1 - par, 1, loop)
                        stack_k(i + 1, 1 - par, 2, loop)
                        for a in range(PARTS):
                            stack_q(i + 1, 1 - par, a, loop)
                        repeat_q(i + 1, 1 - par)
                        load_rows(i + 1, 1 - par, loop)
                    if j == 0 and third and (loop or i > -2):
                        load(i + 2, par, loop)
                    if j == 1 and exists(i - 2, loop):
                        store(i - 2, par)
                    if j == 1 and exists(i - 1, loop):
                        spread_gates(i - 1, 1 - par)
                    if j >= 1 and exists(i - 1, loop):
                        broadcast_gates(i - 1, 1 - par, j - 1)

            steps(sp, step)
            for par in range(2):
                sp.wait_ge(stored[par], 16 * (S // 2 + 1))

        @block.tensor
        def _(pe):
            def claim(s, name, loop=False):
                bank, n = ab(s, name)
                if loop or n > 1:
                    pe.wait_ge(ab_taken[bank], n - 1)
                return bank_ab[bank], ab_ready[bank]

            def transpose_ctx(s, loop=False):
                pe.wait_ge(norm_d, at(NORM, s, "ctx_normed"))
                p, ready = claim(s, "ctxT", loop)
                for b in range(G):
                    mm = nc.tensor.transpose(p[0:L, N * b:N * b + N], cn[:, b, :], ident[0:N, 0:N])
                mm.then_inc(ready, 1)

            def transpose_x(s, loop=False):
                pe.wait_ge(norm_d, at(NORM, s, "x_normed"))
                p, ready = claim(s, "xT", loop)
                for b in range(G):
                    mm = nc.tensor.transpose(p[:, T * b:T * b + T], xn[:, b, :], ident[:, :])
                mm.then_inc(ready, 1)

            def project_keys(s, loop=False):
                bank, n = ab(s, "ctxT")
                pe.wait_ge(ab_taken[bank], n)
                p, ready = claim(s, "k", loop)
                nc.tensor.matmul(p[:, 0:G * N], wk[:, :], cnT[0:L, :], start=True, stop=True).then_inc(ready, 1)

            def project_queries(s, loop=False):
                bank, n = ab(s, "xT")
                pe.wait_ge(ab_taken[bank], n)
                p, ready = claim(s, "q", loop)
                nc.tensor.matmul(p[:, :], wq[:, :], xnT[:, :], start=True, stop=True).then_inc(ready, 1)

            def project_values(s, loop=False):
                p, ready = claim(s, "v", loop)
                for b in range(G):
                    mm = nc.tensor.matmul(p[0:N, D * b:D * b + D], cnT[:, N * b:N * b + N], wv[:, :],
                                          start=True, stop=True)
                mm.then_inc(ready, 1)

            def stacked(s, par, loop=False):
                pe.wait_ge(k_stacked[par], landed(s, par, TERMS))
                pe.wait_ge(q_stacked[par], landed(s, par, Q_DMAS))

            def scores(s, par, j, c, loop=False):
                if j == 0 and c == 0:
                    stacked(s, par, loop)
                h0, h1 = HEADS_S1[c]
                p, ready = claim(s, f"s1{'abc'[c]}{j}", loop)
                for h in range(h0, h1):
                    mm = nc.tensor.matmul(p[:, N * (h - h0):N * (h - h0 + 1)], qs[0:QR, par, h, T * j:T * j + T],
                                          ks[0:QR, par, h, N * j:N * j + N], start=True, stop=True)
                mm.then_inc(ready, 1)

            def max_turn(s, par, j, loop=False):
                pe.wait_ge(max_d, at(MAXP, G * s + j, "lo"))
                p, ready = claim(s, f"mT{j}", loop)
                apart(pe)
                nc.tensor.transpose(p[:, :].bitcast(BF16)[0:PARTS * H, 0:T],
                                    m_parts[:, :, :].rearrange("t a h -> t (a h)"), ident_bf[:, :]).then_inc(ready, 1)

            def scoresT(s, par, j, c, loop=False):
                if not loop and (s, j, c) == (0, 0, 0):
                    pe.wait_ge(ones_in, 16 * 2)
                if c == 0:
                    pe.wait_ge(m_in[j], 16 * s + 16)
                m = NC * (G * s + j) + c
                if loop or m >= 2:
                    pe.wait_ge(p_done, m - 1)
                p = bank_s2[c % 2]
                for h in range(CH * c, CH * c + CH):
                    mm = nc.tensor.matmul(p[0:N, T * (h - CH * c):T * (h - CH * c + 1)],
                                          ks[:, par, h, N * j:N * j + N], qs[:, par, h, T * j:T * j + T],
                                          start=True, stop=True)
                mm.then_inc(s2_ready, 1)

            def values(s, par, j, c, loop=False):
                n = G * s + j
                m = NC * n + c
                if c == 0:
                    pe.wait_ge(split_v, at(SPLIT, s, "lo"))
                    if loop or n > 0:
                        pe.wait_ge(post_d, at(POST, n - 1, "recip"))
                pe.wait_ge(lo_done, m + 1)
                for h in range(CH * c, CH * c + CH):
                    k = T * (h - CH * c)
                    for part in (p_hi, p_lo):
                        mm = nc.tensor.matmul(bank_c[:, VC * h:VC * h + VC], part[:, c, k:k + T],
                                              vs[:, par, j, h, :], start=(h == 0 and part is p_hi),
                                              stop=(part is p_lo), skip_group_check=True)
                mm.then_inc(pv_done, 1)

            def turn(s, par, j, loop=False):
                pe.wait_ge(post_d, at(POST, G * s + j, "normed"))
                p, ready = claim(s, f"turn{j}", loop)
                nc.tensor.transpose(p[:, 0:T], xn2[:, :], ident[:, :]).then_inc(ready, 1)

            def route(s, par, j, loop=False):
                if not loop and (s, j) == (0, 0):
                    pe.wait_ge(experts_in, 16 * 3)
                pe.wait_ge(xT_done, G * s + j + 1)
                p, ready = claim(s, f"route{j}", loop)
                nc.tensor.matmul(p[:, 0:E], xT32[:, j % 2, :], wr[:, :], start=True, stop=True).then_inc(ready, 1)

            def gates_turn(s, loop=False):
                pe.wait_ge(gate_d, at(GATE, s, "gates"))
                p, ready = claim(s, "gates", loop)
                nc.tensor.transpose(p[0:G * E, 0:T], gates[:, :, :].rearrange("t e b -> t (e b)"),
                                    ident[:, :]).then_inc(ready, 1)

            def hidden(s, par, e, loop=False):
                if not loop and (s, e) == (0, 0):
                    pe.wait_ge(experts_made, 3)
                if e == 0:
                    pe.wait_ge(late_d, at(LATE, G * s + G - 1, "x_lo"))
                if loop or E * s + e >= 2:
                    pe.wait_ge(u_done, E * s + e - 1)
                p = bank_h[e % 2]
                nc.tensor.matmul(p[:, :], w1_lo[:, e, :], x_hi[:, par, :], start=True, stop=False)
                nc.tensor.matmul(p[:, :], w1_hi[:, e, :], x_lo[:, par, :], start=False, stop=False)
                nc.tensor.matmul(p[:, :], w1_hi[:, e, :], x_hi[:, par, :], start=False, stop=True).then_inc(h_ready, 1)

            def output(s, par, e, loop=False):
                pe.wait_ge(hs_done, E * s + e + 1)
                if e == 0 and (loop or s > 0):
                    pe.wait_ge(y_added, s)
                for b in range(G):
                    mm = nc.tensor.matmul(bank_y[:, D * b:D * b + D], hs[:, e % 2, T * b:T * b + T], w2s[:, e, :],
                                          start=(e == 0 and b == 0), stop=(e == E - 1), skip_group_check=True)
                mm.then_inc(y_done, 1)

            pe.wait_ge(const_made, CONSTS)
            pe.wait_ge(w_made, WEIGHTS)
            pe.wait_ge(w_in, 16 * HW_WEIGHTS)
            pe.wait_ge(w_in_pool, 16 * POOL_WEIGHTS)

            def step(i, par, loop=False):
                for j, near, nxt, third, ffn in slots(i, par, loop):
                    sf, pf, pending, e = ffn
                    if near[-2]:
                        turn(*near[-2], loop)
                    if pending is not None:
                        output(sf, pf, pending, loop)
                    if near[2]:
                        scores(*near[2], 2, loop)
                    if near[-1]:
                        values(*near[-1], 3, loop)
                    if near[-2]:
                        route(*near[-2], loop)
                    if near[0]:
                        scoresT(*near[0], 1, loop)
                    if e[0] is not None:
                        hidden(sf, pf, e[0], loop)
                    if j == 0 and nxt:
                        project_keys(nxt[0], loop)
                    if e[1] is not None:
                        hidden(sf, pf, e[1], loop)
                    if near[0]:
                        scoresT(*near[0], 2, loop)
                    if j == 1 and nxt:
                        project_values(nxt[0], loop)
                    if near[2]:
                        max_turn(*near[2], loop)
                    if near[0]:
                        values(*near[0], 0, loop)
                    if j == 0 and nxt:
                        project_queries(nxt[0], loop)
                    if e[2] is not None:
                        hidden(sf, pf, e[2], loop)
                    if near[0]:
                        scoresT(*near[0], 3, loop)
                    if e[0] is not None:
                        output(sf, pf, e[0], loop)
                    if j == 1 and exists(i - 1, loop):
                        gates_turn(i - 1, loop)
                    if j == 3 and third:
                        transpose_ctx(third[0], loop)
                    if near[3]:
                        scores(*near[3], 0, loop)
                    if near[1]:
                        scoresT(*near[1], 0, loop)
                    if e[1] is not None:
                        output(sf, pf, e[1], loop)
                    if near[3]:
                        scores(*near[3], 1, loop)
                    if near[0]:
                        values(*near[0], 1, loop)
                    if j == 3 and third:
                        transpose_x(third[0], loop)
                    if near[0]:
                        values(*near[0], 2, loop)

            steps(pe, step)

        @block.scalar
        def _(act):
            def evacuate_xT(s):
                bank, n = ab(s, "xT")
                act.wait_ge(ab_ready[bank], n)
                nc.scalar.activation(xnT[:, :], bank_ab[bank][:, :], ACT.Identity, bias=col(NB_),
                                     scale=col(NG)).then_inc(ab_taken[bank], 1)

            def evacuate_ctxT(s):
                bank, n = ab(s, "ctxT")
                act.wait_ge(ab_ready[bank], n)
                nc.scalar.activation(cnT[0:L, :], bank_ab[bank][0:L, 0:G * N], ACT.Identity, bias=col(TB, L),
                                     scale=col(TG, L)).then_inc(ab_taken[bank], 1)

            def max_store(s, par, j, loop=False):
                bank, k = ab(s, f"mT{j}")
                act.wait_ge(ab_ready[bank], k)
                if j >= 2:
                    act.wait_ge(m_in[j - 2], 16 * s + 16)
                elif loop or s > 0:
                    act.wait_ge(m_in[j + 2], 16 * s)
                nc.scalar.activation(mT[:, j % 2, :], bank_ab[bank][:, :].bitcast(BF16)[0:PARTS * H, 0:T],
                                     ACT.Copy).then_inc(ab_taken[bank], 1)

            def gate_rows(s):
                bank, k = ab(s, "gates")
                act.wait_ge(ab_ready[bank], k)
                nc.scalar.activation(gatesT[:, :], bank_ab[bank][0:G * E, 0:T], ACT.Copy).then_inc(ab_taken[bank], 1)

            def evacuate_k(s, par, loop=False):
                bank, n = ab(s, "k")
                act.wait_ge(ab_ready[bank], n)
                if loop or s > 0:
                    act.wait_ge(k_stacked[1 - par], landed(s - 1, 1 - par, TERMS))
                nc.scalar.activation(k_parts[:, 0, :], bank_ab[bank][:, 0:G * N], ACT.Identity,
                                     bias=col(BK)).then_inc(hi_k, 1)
                nc.scalar.activation(k32[:, :], bank_ab[bank][:, 0:G * N], ACT.Identity,
                                     bias=col(BK)).then_inc(ab_taken[bank], 1)

            def evacuate_q(s, par, loop=False):
                bank, n = ab(s, "q")
                act.wait_ge(ab_ready[bank], n)
                if loop or s > 0:
                    act.wait_ge(q_stacked[1 - par], landed(s - 1, 1 - par, Q_DMAS))
                nc.scalar.activation(q_parts[:, 0, :], bank_ab[bank][:, :], ACT.Identity,
                                     bias=col(BQS)).then_inc(hi_q, 1)
                nc.scalar.activation(q32[:, :], bank_ab[bank][:, :], ACT.Identity,
                                     bias=col(BQS)).then_inc(ab_taken[bank], 1)

            def evacuate_v(s, par, loop=False):
                bank, n = ab(s, "v")
                if loop or s >= 2:
                    act.wait_ge(pv_done, NC * G * (s - 1))
                act.wait_ge(ab_ready[bank], n)
                view = vs[:, par, :, :, 0:HD * PARTS].rearrange("n b h (d a) -> n a (b h) d", a=PARTS)
                nc.scalar.activation(view[:, 0],
                                     bank_ab[bank][0:N, :].rearrange("n (c d) -> n c d", d=HD), ACT.Copy,
                                     scale=col(GX, N))
                if loop or s > 0:
                    act.wait_ge(split_v, at(SPLIT, s - 1, "rest"))
                nc.scalar.activation(v32[:, :, :].rearrange("n b d -> n (b d)"), bank_ab[bank][0:N, :], ACT.Copy,
                                     scale=col(GX, N)).then_inc(ab_taken[bank], 1)

            def evacuate_turned(s, par, j, loop=False):
                bank, n = ab(s, f"turn{j}")
                act.wait_ge(ab_ready[bank], n)
                nc.scalar.activation(xT32[:, j % 2, :], bank_ab[bank][:, 0:T], ACT.Copy).then_inc(xT_done, 1)
                nc.scalar.activation(x_hi[:, par, T * j:T * j + T], bank_ab[bank][:, 0:T],
                                     ACT.Copy).then_inc(ab_taken[bank], 1)

            def exponent(s, par, j, c, loop=False):
                m = NC * (G * s + j) + c
                act.wait_ge(s2_ready, m + 1)
                if loop or m >= LR:
                    act.wait_ge(pv_done, m - LR + 1)
                src = bank_s2[c % 2][0:N, :]
                nc.scalar.activation(p_hi[:, c, :], src, ACT.Exp).then_inc(hi_done, 1)
                nc.scalar.activation(p32[:, c, :], src, ACT.Exp).then_inc(p_done, 1)

            def square(s, e, loop=False):
                n = E * s + e
                act.wait_ge(u_done, n + 1)
                if loop or n >= 2:
                    act.wait_ge(y_done, n - 1)
                nc.scalar.activation(hs[:, e % 2, :], u[:, e % 2, :], ACT.Square).then_inc(hs_done, 1)

            def gate_exp(s):
                act.wait_ge(gate_d, at(GATE, s, "diff"))
                nc.scalar.activation(gt[:, 1, :], gt[:, 0, :], ACT.Exp).then_inc(gate_e, 1)
                nc.scalar.activation(gt[:, 2, :], gt[:, 0, :], ACT.Exp, scale=0.5).then_inc(gate_e, 1)

            for dst, src in ((col(NG), norm_g.rearrange("(n o) -> n o", o=1)),
                             (col(NB_), norm_b.rearrange("(n o) -> n o", o=1))):
                with nc.allow_non_contiguous_dma(reason="short vectors"):
                    act.dma_start(dst, src).then_inc(w_in, 16)
            act.wait_ge(w_in, 16 * HW_WEIGHTS)
            act.wait_ge(w_in_pool, 16 * POOL_WEIGHTS)
            nc.scalar.activation(vec[:, GX:GX + 2], vec[:, GX:GX + 2], ACT.Tanh).then_inc(tanh_done, 1)
            act.wait_ge(tanh_done, 1)
            act.wait_ge(w_made, WEIGHTS)

            def step(i, par, loop=False):
                for j, near, nxt, third, ffn in slots(i, par, loop):
                    sf, pf, pending, e = ffn
                    if near[0]:
                        exponent(*near[0], 1, loop)
                    if j == 1 and exists(i - 1, loop):
                        gate_exp(i - 1)
                    if j == 0 and nxt:
                        evacuate_k(*nxt, loop)
                    if j == 1 and nxt:
                        evacuate_v(*nxt, loop)
                    if e[0] is not None:
                        square(sf, e[0], loop)
                    if near[2]:
                        max_store(*near[2], loop)
                    if near[0]:
                        exponent(*near[0], 2, loop)
                    if e[1] is not None:
                        square(sf, e[1], loop)
                    if j == 0 and nxt:
                        evacuate_q(*nxt, loop)
                    if j == 3 and third:
                        evacuate_ctxT(third[0])
                    if near[0]:
                        exponent(*near[0], 3, loop)
                    if e[2] is not None:
                        square(sf, e[2], loop)
                    if j == 1 and exists(i - 1, loop):
                        gate_rows(i - 1)
                    if j == 3 and third:
                        evacuate_xT(third[0])
                    if near[-1]:
                        evacuate_turned(*near[-1], loop)
                    if near[1]:
                        exponent(*near[1], 0, loop)

            steps(act, step)

        @block.vector
        def _(dve):
            def stats(s, par, loop=False):
                dve.wait_ge(ctx_in[par], landed(s, par))
                for b in range(G):
                    ins = nc.vector.bn_stats(c_st[:, b, :], ctx_sb[:, par, b, :])
                ins.then_inc(stats_d, 1)
                yield
                dve.wait_ge(x_in[par], landed(s, par))
                for b in range(G):
                    ins = nc.vector.bn_stats(x_st[:, b, :], x_sb[:, par, b, :])
                ins.then_inc(stats_d, 1)
                yield
                dve.wait_ge(stats_d, at(STATS, s, "x_stats"))
                apart(dve)
                for b in range(G):
                    ins = nc.vector.bn_aggr(c_mv[:, b, :], c_st[:, b, :])
                ins.then_inc(stats_d, 1)
                for b in range(G):
                    ins = nc.vector.bn_aggr(x_mv[:, b, :], x_st[:, b, :])
                ins.then_inc(stats_d, 1)
                yield

            def normalise_ctx(s, par, loop=False):
                dve.wait_ge(norm_p, at(NORM_P, s, "crstd"))
                for b in range(G):
                    ins = nc.vector.tensor_scalar(cn[:, b, :], ctx_sb[:, par, b, :], c_mv[:, b, 0:1],
                                                  nrm[0:N, 1, b:b + 1], ALU.subtract, ALU.mult)
                    if b == G - 1:
                        ins.then_inc(norm_d, 1)
                    if b % 2:
                        yield

            def normalise_x(s, par, loop=False):
                dve.wait_ge(norm_p, at(NORM_P, s, "rstd"))
                for b in range(G):
                    ins = nc.vector.tensor_scalar(xn[:, b, :], x_sb[:, par, b, :], x_mv[:, b, 0:1],
                                                  nrm[:, 3, b:b + 1], ALU.subtract, ALU.mult)
                    if b == G - 1:
                        ins.then_inc(norm_d, 1)
                    if b % 2:
                        yield

            def split(s, done, src, rest, parts):
                nc.vector.tensor_tensor(rest, src, parts[0], ALU.subtract).then_inc(done, 1)
                yield
                dve.wait_ge(done, at(SPLIT, s, "rest"))
                nc.vector.tensor_copy(parts[1], rest).then_inc(done, 1)
                yield
                dve.wait_ge(done, at(SPLIT, s, "mid"))
                nc.vector.tensor_tensor(parts[2], rest, parts[1], ALU.subtract).then_inc(done, 1)
                yield

            def split_keys(s, par, loop=False):
                bank, n = ab(s, "k")
                dve.wait_ge(ab_taken[bank], n)
                yield from split(s, split_k, k32[:, :], k_rest[:, :], [k_parts[:, a, :] for a in range(PARTS)])

            def split_queries(s, par, loop=False):
                bank, n = ab(s, "q")
                dve.wait_ge(ab_taken[bank], n)
                yield from split(s, split_q, q32[:, :], q_rest[:, :], [q_parts[:, a, :] for a in range(PARTS)])

            def split_values(s, par, loop=False):
                view = vs[:, par, :, :, 0:HD * PARTS].rearrange("n b h (d a) -> n a (b h) d", a=PARTS)
                v = v32[:, :, :].rearrange("n b (h d) -> n (b h) d", d=HD)
                rest = v_rest[:, :, :].rearrange("n b (h d) -> n (b h) d", d=HD)
                bank, n = ab(s, "v")
                dve.wait_ge(ab_taken[bank], n)
                yield from split(s, split_v, v, rest, [view[:, a] for a in range(PARTS)])

            def maximum(s, par, j, loop=False):
                n = G * s + j
                for c, (h0, h1) in enumerate(HEADS_S1):
                    bank, k = ab(s, f"s1{'abc'[c]}{j}")
                    dve.wait_ge(ab_ready[bank], k)
                    nc.vector.tensor_reduce(negm[:, h0:h1],
                                            bank_ab[bank][:, 0:N * (h1 - h0)].rearrange("t (h n) -> t h n", n=N),
                                            AX.X, ALU.max, negate=True).then_inc(ab_taken[bank], 1)
                    yield
                for bank, k in {b: k for b, k in (ab(s, f"s1{u}{j}") for u in "abc")}.items():
                    dve.wait_ge(ab_taken[bank], k)
                nc.vector.tensor_copy(m_parts[:, 0, :], negm[:, :]).then_inc(max_d, 1)
                yield
                dve.wait_ge(max_d, at(MAXP, n, "hi"))
                nc.vector.tensor_tensor(m_rest[:, :], negm[:, :], m_parts[:, 0, :], ALU.subtract).then_inc(max_d, 1)
                yield
                dve.wait_ge(max_d, at(MAXP, n, "rest"))
                nc.vector.tensor_copy(m_parts[:, 1, :], m_rest[:, :]).then_inc(max_d, 1)
                yield
                dve.wait_ge(max_d, at(MAXP, n, "mid"))
                nc.vector.tensor_tensor(m_parts[:, 2, :], m_rest[:, :], m_parts[:, 1, :],
                                        ALU.subtract).then_inc(max_d, 1)
                yield

            def attended(s, par, j, loop=False):
                n = G * s + j
                dve.wait_ge(pv_done, NC * n + NC)
                view = bank_c[:, 0:VC * H].rearrange("t (h v) -> t h v", v=VC)
                nc.vector.tensor_reduce(o[:, :].rearrange("t (h d) -> t h d", d=HD),
                                        view[:, :, 0:HD * PARTS].rearrange("t h (d a) -> t h d a", a=PARTS),
                                        AX.X, ALU.add).then_inc(post_d, 1)
                nc.vector.reciprocal(rden[:, :].rearrange("t (h o) -> t h o", o=1),
                                     view[:, :, HD * PARTS:VC]).then_inc(post_d, 1)
                yield
                dve.wait_ge(post_d, at(POST, n, "recip"))
                nc.vector.tensor_tensor(o[:, :].rearrange("t (h d) -> t h d", d=HD),
                                        o[:, :].rearrange("t (h d) -> t h d", d=HD),
                                        rden[:, :].rearrange("t (h o) -> t h o", o=1).broadcast_to([T, H, HD]),
                                        ALU.mult).then_inc(post_d, 1)
                yield
                if j == 0:
                    dve.wait_ge(res_in[par], landed(s, par))
                    if loop or s >= 2:
                        dve.wait_ge(y_added, s - 1)
                dve.wait_ge(post_d, at(POST, n, "scaled"))
                nc.vector.tensor_tensor(x1[:, par, j, :], x_res[:, par, j, :], o[:, :], ALU.add).then_inc(post_d, 1)
                yield
                dve.wait_ge(post_d, at(POST, n, "x1"))
                nc.vector.bn_stats(st2[:, :], x1[:, par, j, :]).then_inc(post_d, 1)
                yield
                dve.wait_ge(post_d, at(POST, n, "stats"))
                apart(dve)
                nc.vector.bn_aggr(mv2[:, :], st2[:, :]).then_inc(post_d, 1)
                yield

            def normalise2(s, par, j):
                n = G * s + j
                dve.wait_ge(post_p, at(POST_P, n, "rstd"))
                nc.vector.tensor_scalar(xn2[:, :], x1[:, par, j, :], mv2[:, 0:1], rs2[:, 1:2], ALU.subtract,
                                        ALU.mult).then_inc(post_d, 1)

            def low_x(s, par, j):
                bank, k = ab(s, f"turn{j}")
                dve.wait_ge(ab_taken[bank], k)
                nc.vector.tensor_tensor(x_lo[:, par, T * j:T * j + T], xT32[:, j % 2, :],
                                        x_hi[:, par, T * j:T * j + T].bitcast(F32), ALU.subtract).then_inc(late_d, 1)

            def routed(s, par, j):
                n = G * s + j
                bank, k = ab(s, f"route{j}")
                dve.wait_ge(ab_ready[bank], k)
                apart(dve)
                nc.vector.max(top[:, j, :], bank_ab[bank][:, 0:E]).then_inc(late_d, 1)
                nc.vector.tensor_copy(logits[:, j, :], bank_ab[bank][:, 0:E]).then_inc(ab_taken[bank], 1)

            def gate(s):
                bank, k = ab(s, "route3")
                dve.wait_ge(ab_taken[bank], k)
                dve.wait_ge(late_d, at(LATE, G * s + G - 1, "top"))
                apart(dve)
                nc.vector.tensor_tensor(gt[:, 0, :], top[:, :, 1], top[:, :, 0], ALU.subtract).then_inc(gate_d, 1)
                for b in range(G):
                    ins = nc.vector.max_index(index[:, b, :], top[:, b, :], logits[:, b, :])
                ins.then_inc(gate_d, 1)
                yield
                dve.wait_ge(gate_e, 2 * s + 1)
                nc.vector.tensor_scalar(gt[:, 3, :], gt[:, 1, :], 1.0, None, ALU.add).then_inc(gate_d, 1)
                yield
                dve.wait_ge(gate_d, at(GATE, s, "index"))
                nc.vector.tensor_copy(idx_f[:, :, :], index[:, :, 0:2]).then_inc(gate_d, 1)
                yield
                dve.wait_ge(gate_d, at(GATE, s, "idx_f"))
                for which, dst in ((0, eq1), (1, eq2)):
                    nc.vector.tensor_tensor(dst[:, :, :], iota[:, :, :],
                                            idx_f[:, :, which:which + 1].broadcast_to([T, G, E]),
                                            ALU.is_equal).then_inc(gate_d, 1)
                yield
                dve.wait_ge(gate_e, 2 * s + 2)
                dve.wait_ge(gate_d, at(GATE, s, "eq2"))
                nc.vector.tensor_tensor(eq2[:, :, :], eq2[:, :, :],
                                        gt[:, 2, :].rearrange("t (b o) -> t b o", o=1).broadcast_to([T, G, E]),
                                        ALU.mult).then_inc(gate_d, 1)
                yield
                dve.wait_ge(gate_d, at(GATE, s, "second"))
                nc.vector.tensor_tensor(eq1[:, :, :], eq1[:, :, :], eq2[:, :, :], ALU.add).then_inc(gate_d, 1)
                yield
                dve.wait_ge(gate_p, s + 1)
                dve.wait_ge(gate_d, at(GATE, s, "both"))
                nc.vector.tensor_tensor(gates[:, :, :].rearrange("t e b -> t b e"), eq1[:, :, :],
                                        gt[:, 4, :].rearrange("t (b o) -> t b o", o=1).broadcast_to([T, G, E]),
                                        ALU.mult).then_inc(gate_d, 1)
                yield

            def gated(s, par, e, loop=False):
                n = E * s + e
                if e in GATE_CUTS:
                    dve.wait_ge(g_in[par][GATE_CUTS.index(e)], landed(s, par))
                dve.wait_ge(h_ready, n + 1)
                if loop or n >= 2:
                    dve.wait_ge(hs_done, n - 1)
                nc.vector.scalar_tensor_tensor(out=u[:, e % 2, :], in0=bank_h[e % 2][:, :], scalar=0.0,
                                               in1=gb[:, par, e, :], op0=ALU.max, op1=ALU.mult).then_inc(u_done, 1)

            def finish(s, par, loop=False):
                dve.wait_ge(y_done, E * s + E)
                dve.wait_ge(stored[par], landed(s, par))
                nc.vector.tensor_tensor(y_out[:, par].rearrange("t b d -> t (b d)"),
                                        x1[:, par].rearrange("t b d -> t (b d)"), bank_y[:, :],
                                        ALU.add).then_inc(y_added, 1)

            def chained(*stages):
                for stage in stages:
                    yield from stage

            def take(stage, count=1):
                for _ in range(count):
                    next(stage, None)

            nc.vector.memset(ones[:, :], 1.0).then_inc(ones_made, 1)
            nc.vector.memset(cnT[L:L + 1, :], 1.0).then_inc(ones_made, 1)
            nc.vector.memset(vs[:, :, :, :, HD * PARTS:VC], 1.0).then_inc(ones_made, 1)
            take(stats(0, 0), 3)
            dve.wait_ge(w_in, 16 * HW_WEIGHTS)
            nc.vector.tensor_copy(wk[:, :].rearrange("c (d h) -> c d h", d=HD),
                                  wk_in[:, :].rearrange("c (h d) -> c d h", d=HD)).then_inc(w_made, 1)
            nc.vector.tensor_scalar(wq[:, :].rearrange("c (d h) -> c d h", d=HD),
                                    wq_in[:, :].rearrange("c (h d) -> c d h", d=HD), SCALE, None,
                                    ALU.mult).then_inc(w_made, 1)
            dve.wait_ge(w_in_pool, 16 * POOL_WEIGHTS)
            nc.vector.tensor_scalar(col(BQS), col(BQ), SCALE, None, ALU.mult).then_inc(w_made, 1)
            dve.wait_ge(const_made, CONSTS)
            nc.vector.tensor_copy(ident_bf[:, :], ident[:, :]).then_inc(w_made, 1)

            def prepare_experts():
                dve.wait_ge(experts_in, 16 * 3)
                nc.vector.tensor_copy(w1_hi[:, :, :], w1_in[:, :, :]).then_inc(experts_made, 1)
                dve.wait_ge(tanh_done, 1)
                nc.vector.tensor_scalar(w2s[:, :, :], w2_in[:, :, :], col(GF), None, ALU.mult)\
                    .then_inc(experts_made, 1)
                dve.wait_ge(experts_made, 1)
                nc.vector.tensor_tensor(w1_lo[:, :, :], w1_in[:, :, :], w1_hi[:, :, :].bitcast(F32),
                                        ALU.subtract).then_inc(experts_made, 1)

            def step(i, par, loop=False):
                for j, near, nxt, third, ffn in slots(i, par, loop):
                    sf, pf, pending, e = ffn
                    none = iter(())
                    top_scores = maximum(*near[2], loop) if near[2] else none
                    post = attended(*near[-1], loop) if near[-1] else none
                    gates_now = j == 1 and exists(i - 1, loop)
                    gating = gate(i - 1) if gates_now else none
                    prepare = none
                    if j == 0 and nxt:
                        prepare = chained(split_keys(*nxt, loop), split_queries(*nxt, loop))
                    if j == 1 and nxt:
                        prepare = split_values(*nxt, loop)
                    if j == 2 and third and (loop or i > -2):
                        prepare = stats(*third, loop)
                    if j == 3 and third:
                        prepare = chained(normalise_ctx(*third, loop), normalise_x(*third, loop))
                    if j == 3 and not loop and i == -1:
                        prepare_experts()
                    take(top_scores)
                    take(top_scores)
                    take(top_scores)
                    if j == 1 and exists(i - 2, loop):
                        finish(sf, pf, loop)
                    take(post)
                    take(top_scores)
                    if near[-2]:
                        routed(*near[-2])
                    take(top_scores)
                    take(post)
                    if near[-2]:
                        low_x(*near[-2])
                    take(gating)
                    take(gating)
                    take(top_scores)
                    if e[0] is not None:
                        gated(sf, pf, e[0], loop)
                    take(gating)
                    take(post)
                    take(top_scores)
                    take(post)
                    take(gating)
                    take(gating)
                    take(prepare)
                    take(post)
                    take(prepare)
                    if e[1] is not None:
                        gated(sf, pf, e[1], loop)
                    if e[2] is not None:
                        gated(sf, pf, e[2], loop)
                    take(prepare)
                    take(prepare)
                    take(gating)
                    take(gating)
                    take(prepare)
                    take(gating)
                    take(prepare)
                    if near[-1]:
                        normalise2(*near[-1])
                    take(prepare, SLOTS)

            steps(dve, step)

        @block.gpsimd
        def _(pool):
            def norm_rstd(s, which):
                pool.wait_ge(stats_d, at(STATS, s, f"{which}_moments"))
                apart(pool)
                n, mv, k, scale, eps, names = {"ctx": (N, c_mv, 0, 1.0, EPS, ("cvar_eps", "crstd")),
                                               "x": (T, x_mv, 2, 1.0 + EPS, EPS * EPS, ("var_eps", "rstd"))}[which]
                nc.gpsimd.tensor_scalar(nrm[0:n, k, :], mv[:, :, 1], scale, eps, ALU.mult, ALU.add).then_inc(norm_p, 1)
                pool.wait_ge(norm_p, at(NORM_P, s, names[0]))
                nc.gpsimd.tensor_tensor(nrm[0:n, k + 1, :], nrm[0:n, k, :], neg_half[0:n, :],
                                        ALU.pow).then_inc(norm_p, 1)

            def low_part(s, par, j, c):
                m = NC * (G * s + j) + c
                pool.wait_ge(hi_done, m + 1)
                pool.wait_ge(p_done, m + 1)
                nc.gpsimd.tensor_tensor(p_lo[:, c, :], p32[:, c, :], p_hi[:, c, :],
                                        ALU.subtract).then_inc(lo_done, 1)

            def rstd(s, par, j):
                n = G * s + j
                pool.wait_ge(post_d, at(POST, n, "moments"))
                apart(pool)
                nc.gpsimd.tensor_scalar(rs2[:, 0:1], mv2[:, 1:2], EPS, None, ALU.add).then_inc(post_p, 1)
                pool.wait_ge(post_p, at(POST_P, n, "var_eps"))
                nc.gpsimd.tensor_tensor(rs2[:, 1:2], rs2[:, 0:1], neg_half[:, 0:1], ALU.pow).then_inc(post_p, 1)

            def gate_roots(s):
                pool.wait_ge(gate_d, at(GATE, s, "den"))
                nc.gpsimd.tensor_tensor(gt[:, 4, :], gt[:, 3, :], neg_half[:, :], ALU.pow).then_inc(gate_p, 1)

            def load_experts():
                for dst, src in ((w1_in[:, :, :], w1.rearrange("e c d -> c e d")),
                                 (w2_in[:, :, :], w2.rearrange("e d c -> d e c")), (wr[:, :], w_router)):
                    pool.dma_start(dst, src).then_inc(experts_in, 16)

            nc.gpsimd.memset(ident[:, :], 0.0).then_inc(const_made, 1)
            pool.wait_ge(const_made, 1)
            nc.gpsimd.affine_select(out=ident[:, :], in_=ident[:, :], compare_op=ALU.not_equal, fill=1.0, base=0,
                                    pattern=[[-1, 128]], channel_multiplier=1).then_inc(const_made, 1)
            nc.gpsimd.memset(neg_half[:, :], -0.5).then_inc(const_made, 1)
            for e in range(E):
                nc.gpsimd.memset(iota[:, :, e], float(e)).then_inc(const_made, 1)
            for dst, src in ((col(BQ), bq.rearrange("(h d o) -> d h o", d=HD, o=1)),
                             (col(GX), g_xattn.rearrange("(n o) -> n o", o=1).broadcast_to([128, 1])),
                             (col(GF), g_ffn.rearrange("(n o) -> n o", o=1).broadcast_to([128, 1]))):
                with nc.allow_non_contiguous_dma(reason="short vectors"):
                    pool.dma_start(dst, src).then_inc(w_in_pool, 16)
            for par in range(2):
                nc.gpsimd.memset(y_out[:, par, :, :], 0.0).then_inc(stored[par], 16)

            def step(i, par, loop=False):
                for j, near, nxt, third, ffn in slots(i, par, loop):
                    if not loop and (i, j) == (-1, 0):
                        load_experts()
                    if j == 3 and third:
                        norm_rstd(third[0], "ctx")
                    if near[0]:
                        low_part(*near[0], 0)
                    if j == 3 and third:
                        norm_rstd(third[0], "x")
                    if j == 1 and exists(i - 1, loop):
                        gate_roots(i - 1)
                    if near[0]:
                        low_part(*near[0], 1)
                    if near[-1]:
                        rstd(*near[-1])
                    if near[0]:
                        low_part(*near[0], 2)
                    if near[0]:
                        low_part(*near[0], 3)

            steps(pool, step)


_INS = ["x", "ctx_768", "g_xattn", "g_ffn", "L0_xattn_norm_g", "L0_xattn_norm_b", "L0_xattn_tnorm_g",
        "L0_xattn_tnorm_b", "L0_xattn_Wq", "L0_xattn_bq", "L0_xattn_Wk", "L0_xattn_bk", "L0_xattn_Wv",
        "L0_xattn_bv", "L0_ffn_w_router", "L0_ffn_w1", "L0_ffn_w2"]


def kernel(**inputs):
    import numpy as _np
    import concourse.bacc as _bacc
    from concourse import mybir as _mybir
    from concourse.bass_utils import run_bass_kernel_spmd as _run

    nc = _bacc.Bacc("TRN2", target_bir_lowering=False, num_devices=1)
    arrays, args = {}, []
    for name in _INS:
        a = _np.ascontiguousarray(inputs[name])
        arrays[f"in_{name}_dram"] = a
        args.append(nc.dram_tensor(f"in_{name}_dram", a.shape, _mybir.dt.from_np(a.dtype), kind="ExternalInput").ap())
    args.append(nc.dram_tensor("out_0_dram", tuple(inputs["x"].shape), _mybir.dt.float32, kind="ExternalOutput").ap())
    flamingo_kernel(nc, *args)
    r = _run(nc, [arrays], core_ids=[0])
    return r.results[0]["out_0_dram"]
```
